# Optimizing a Trainium2 kernel written in Bass

```python
import numpy as np
import jax
import jax.numpy as jnp

def _softmax(x, axis=-1):
    return jax.nn.softmax(x, axis=axis)

def _gelu(x):
    return jax.nn.gelu(x, approximate=True)

def _silu(x):
    return jax.nn.silu(x)

def _sigmoid(x):
    return jax.nn.sigmoid(x)

def _layernorm(x, axis=-1, eps=1e-05):
    m = jnp.mean(x, axis=axis, keepdims=True)
    v = jnp.var(x, axis=axis, keepdims=True)
    return (x - m) / jnp.sqrt(v + eps)

def _scatter_add(tgt, idx, src, axis=0):
    return tgt.at[idx].add(src)

def _segment_sum(src, seg, n):
    return jax.ops.segment_sum(src, seg, n)
kernel_name = 'mk_xattn_seq_d4_seqx_r8_e6885d'

def setup_inputs(seed: int=0):
    np.random.seed(seed)
    _w = jnp.asarray

    def _rec_inputs():
        import jax
        import jax.numpy as jnp
        _rk = jax.random.key(seed)
        x = -0.0001233 + 1 * jax.random.normal(jax.random.fold_in(_rk, 1), (64, 128, 160), jnp.float32)
        _lenS = 128 - jax.random.randint(jax.random.fold_in(_rk, 7), (64,), 0, max(1, 128 // 4) + 1, jnp.int32)
        _lenS2 = 77 - jax.random.randint(jax.random.fold_in(_rk, 8), (64,), 0, max(1, 77 // 4) + 1, jnp.int32)
        _ctx_2048P = jax.random.normal(jax.random.fold_in(_rk, 11), (64, 16, 256), jnp.float32)
        _ctx_2048c = jax.random.dirichlet(jax.random.fold_in(_rk, 511), 0.3 * jnp.ones((16,), jnp.float32), (64, 77))
        _ctx_2048t = jnp.einsum('bsk,bkd->bsd', _ctx_2048c, _ctx_2048P)
        _ctx_2048t = _ctx_2048t * jax.lax.rsqrt(jnp.mean(jnp.square(_ctx_2048t)) + 1e-12) * 0.953939
        ctx_2048 = 0.00266749 + 0.998873 * (_ctx_2048t + 0.3 * jax.random.normal(jax.random.fold_in(_rk, 611), (64, 77, 256), jnp.float32))
        fside_S_0 = jax.random.uniform(jax.random.fold_in(_rk, 12), (128,), jnp.float32, 0.0, 0.999707)
        return (x, ctx_2048, fside_S_0)
    x, ctx_2048, fside_S_0 = _rec_inputs()

    def _L0_xattn_setup():
        import jax, jax.numpy as jnp
        import numpy as np
        B, S, C = (2, 512, 160)
        CA = 256
        HEADS = 20
        HD = C // HEADS
        N_TXT, N_OBJ, N_OTH, N_IP = (77, 4, 4, 16)
        SCALE_OBJ = SCALE_OTH = SCALE_IP = 1.0
        RESCALE = 1.0

        def _heads(x):
            b, l, _ = x.shape
            return x.reshape(b, l, HEADS, HD).transpose(0, 2, 1, 3)

        def _merge(x):
            b, h, l, d = x.shape
            return x.transpose(0, 2, 1, 3).reshape(b, l, h * d)

        def _sdpa(q, k, v):
            scale = 1.0 / np.sqrt(HD).astype(np.float32)
            s = jnp.einsum('bhqd,bhkd->bhqk', q, k) * scale
            p = jax.nn.softmax(s, axis=-1)
            return jnp.einsum('bhqk,bhkd->bhqd', p, v)
        key = jax.random.key(seed)
        ks = jax.random.split(key, 16)
        g = lambda k, shp, fan: jax.random.normal(k, shp, jnp.float32) / np.sqrt(fan).astype(np.float32)
        return {'hidden_states': jax.random.normal(ks[0], (B, S, C), jnp.float32), 'encoder_hidden_states': jax.random.normal(ks[1], (B, N_TXT + N_OBJ + N_OTH + N_IP, CA), jnp.float32), 'to_q_w': g(ks[2], (C, C), C), 'to_k_w': g(ks[3], (CA, C), CA), 'to_v_w': g(ks[4], (CA, C), CA), 'to_k_object_w': g(ks[5], (CA, C), CA), 'to_v_object_w': g(ks[6], (CA, C), CA), 'to_k_others_w': g(ks[7], (CA, C), CA), 'to_v_others_w': g(ks[8], (CA, C), CA), 'to_k_ip_w': g(ks[9], (CA, C), CA), 'to_v_ip_w': g(ks[10], (CA, C), CA), 'to_out_w': g(ks[11], (C, C), C), 'to_out_b': jnp.zeros((C,), jnp.float32)}
    _L0_xattn_all = _L0_xattn_setup()
    _L0_xattn_in = {k: v for k, v in _L0_xattn_all.items() if k in ('to_q_w', 'to_k_w', 'to_v_w', 'to_k_object_w', 'to_v_object_w', 'to_k_others_w', 'to_v_others_w', 'to_k_ip_w', 'to_v_ip_w', 'to_out_w', 'to_out_b')}
    del _L0_xattn_all

    def _L1_xattn_setup():
        import jax, jax.numpy as jnp
        import numpy as np
        import math
        HEADS = 20
        NUM_TOKENS = 4
        SEM_SCALE = 0.5
        IP_SCALE = 1.0
        TEXT_LEN = 77

        def _split_heads(x, B, H, D):
            return x.reshape(B, -1, H, D).transpose(0, 2, 1, 3)
        key = jax.random.key(seed)
        ks = jax.random.split(key, 10)
        B, S, C, CD = (4, 512, 160, 256)

        def g(k, shape, std=1.0):
            return jax.random.normal(k, shape, dtype=jnp.float32) * std
        return {'hidden_states': g(ks[0], (B, S, C)), 'encoder_hidden_states': g(ks[1], (B, TEXT_LEN + NUM_TOKENS, CD)), 'spatial_mask': jax.random.uniform(ks[2], (S,), dtype=jnp.float32), 'Wq': g(ks[3], (C, C), 1.0 / math.sqrt(C)), 'Wk': g(ks[4], (CD, C), 1.0 / math.sqrt(CD)), 'Wv': g(ks[5], (CD, C), 1.0 / math.sqrt(CD)), 'Wk_ip': g(ks[6], (CD, C), 1.0 / math.sqrt(CD)), 'Wv_ip': g(ks[7], (CD, C), 1.0 / math.sqrt(CD)), 'Wout': g(ks[8], (C, C), 1.0 / math.sqrt(C)), 'bout': jnp.zeros((C,), dtype=jnp.float32)}
    _L1_xattn_all = _L1_xattn_setup()
    _L1_xattn_in = {k: v for k, v in _L1_xattn_all.items() if k in ('Wq', 'Wk', 'Wv', 'Wk_ip', 'Wv_ip', 'Wout', 'bout')}
    del _L1_xattn_all

    def _L2_xattn_setup():
        import jax, jax.numpy as jnp
        import numpy as np
        NUM_HEADS = 20
        TEXT_LEN = 77
        IP_SCALE = 1.0

        def _attend(q, k, v, sm_scale):
            scores = jnp.einsum('bhsd,bhld->bhsl', q, k) * sm_scale
            probs = jax.nn.softmax(scores, axis=-1)
            return jnp.einsum('bhsl,bhld->bhsd', probs, v)

        def _split_heads(x, h):
            b, s, c = x.shape
            return x.reshape(b, s, h, c // h).transpose(0, 2, 1, 3)

        def _merge_heads(x):
            b, h, s, d = x.shape
            return x.transpose(0, 2, 1, 3).reshape(b, s, h * d)
        key = jax.random.key(seed)
        ks = jax.random.split(key, 8)
        B, S, C, CC, L = (8, 512, 160, 256, TEXT_LEN + 4)
        sd_q = 1.0 / np.sqrt(C)
        sd_kv = 1.0 / np.sqrt(CC)
        return {'hidden_states': jax.random.normal(ks[0], (B, S, C), jnp.float32), 'encoder_hidden_states': jax.random.normal(ks[1], (B, L, CC), jnp.float32), 'Wq': jax.random.normal(ks[2], (C, C), jnp.float32) * sd_q, 'Wk': jax.random.normal(ks[3], (C, CC), jnp.float32) * sd_kv, 'Wv': jax.random.normal(ks[4], (C, CC), jnp.float32) * sd_kv, 'Wk_ip': jax.random.normal(ks[5], (C, CC), jnp.float32) * sd_kv, 'Wv_ip': jax.random.normal(ks[6], (C, CC), jnp.float32) * sd_kv, 'Wo': jax.random.normal(ks[7], (C, C), jnp.float32) * sd_q, 'bo': jnp.zeros((C,), jnp.float32)}
    _L2_xattn_all = _L2_xattn_setup()
    _L2_xattn_in = {k: v for k, v in _L2_xattn_all.items() if k in ('Wq', 'Wk', 'Wv', 'Wk_ip', 'Wv_ip', 'Wo', 'bo')}
    del _L2_xattn_all

    def _L3_xattn_setup():
        import jax, jax.numpy as jnp
        import numpy as np
        HEADS = 20
        NUM_TOKENS = 4
        IP_SCALE = 1.0
        SEM_SCALE = 0.5
        RESCALE = 1.0
        EPS = 1e-12

        def _l2norm(x, axis=-1):
            n = jnp.sqrt(jnp.sum(x * x, axis=axis, keepdims=True))
            return x / jnp.maximum(n, EPS)
        key = jax.random.key(seed)
        ks = jax.random.split(key, 10)
        B, S, C = (2, 128, 160)
        T, E = (81, 256)
        inp = {'hidden_states': jax.random.normal(ks[0], (B, S, C), jnp.float32), 'encoder_hidden_states': jax.random.normal(ks[1], (B, T, E), jnp.float32), 'spatial_mask': jax.random.uniform(ks[2], (S,), jnp.float32), 'W_q': jax.random.normal(ks[3], (C, C), jnp.float32) * C ** (-0.5), 'W_k': jax.random.normal(ks[4], (E, C), jnp.float32) * E ** (-0.5), 'W_v': jax.random.normal(ks[5], (E, C), jnp.float32) * E ** (-0.5), 'W_k_ip': jax.random.normal(ks[6], (E, C), jnp.float32) * E ** (-0.5), 'W_v_ip': jax.random.normal(ks[7], (E, C), jnp.float32) * E ** (-0.5), 'W_out': jax.random.normal(ks[8], (C, C), jnp.float32) * C ** (-0.5), 'b_out': jnp.zeros((C,), jnp.float32)}
        return inp
    _L3_xattn_all = _L3_xattn_setup()
    _L3_xattn_in = {k: v for k, v in _L3_xattn_all.items() if k in ('W_q', 'W_k', 'W_v', 'W_k_ip', 'W_v_ip', 'W_out', 'b_out')}
    del _L3_xattn_all
    return {'x': x, 'ctx_2048': ctx_2048, 'fside_S_0': fside_S_0, 'L0_xattn_to_q_w': _L0_xattn_in['to_q_w'], 'L0_xattn_to_k_w': _L0_xattn_in['to_k_w'], 'L0_xattn_to_v_w': _L0_xattn_in['to_v_w'], 'L0_xattn_to_k_object_w': _L0_xattn_in['to_k_object_w'], 'L0_xattn_to_v_object_w': _L0_xattn_in['to_v_object_w'], 'L0_xattn_to_k_others_w': _L0_xattn_in['to_k_others_w'], 'L0_xattn_to_v_others_w': _L0_xattn_in['to_v_others_w'], 'L0_xattn_to_k_ip_w': _L0_xattn_in['to_k_ip_w'], 'L0_xattn_to_v_ip_w': _L0_xattn_in['to_v_ip_w'], 'L0_xattn_to_out_w': _L0_xattn_in['to_out_w'], 'L0_xattn_to_out_b': _L0_xattn_in['to_out_b'], 'L1_xattn_Wq': _L1_xattn_in['Wq'], 'L1_xattn_Wk': _L1_xattn_in['Wk'], 'L1_xattn_Wv': _L1_xattn_in['Wv'], 'L1_xattn_Wk_ip': _L1_xattn_in['Wk_ip'], 'L1_xattn_Wv_ip': _L1_xattn_in['Wv_ip'], 'L1_xattn_Wout': _L1_xattn_in['Wout'], 'L1_xattn_bout': _L1_xattn_in['bout'], 'L2_xattn_Wq': _L2_xattn_in['Wq'], 'L2_xattn_Wk': _L2_xattn_in['Wk'], 'L2_xattn_Wv': _L2_xattn_in['Wv'], 'L2_xattn_Wk_ip': _L2_xattn_in['Wk_ip'], 'L2_xattn_Wv_ip': _L2_xattn_in['Wv_ip'], 'L2_xattn_Wo': _L2_xattn_in['Wo'], 'L2_xattn_bo': _L2_xattn_in['bo'], 'L3_xattn_W_q': _L3_xattn_in['W_q'], 'L3_xattn_W_k': _L3_xattn_in['W_k'], 'L3_xattn_W_v': _L3_xattn_in['W_v'], 'L3_xattn_W_k_ip': _L3_xattn_in['W_k_ip'], 'L3_xattn_W_v_ip': _L3_xattn_in['W_v_ip'], 'L3_xattn_W_out': _L3_xattn_in['W_out'], 'L3_xattn_b_out': _L3_xattn_in['b_out']}

def reference(x, ctx_2048, fside_S_0, L0_xattn_to_q_w, L0_xattn_to_k_w, L0_xattn_to_v_w, L0_xattn_to_k_object_w, L0_xattn_to_v_object_w, L0_xattn_to_k_others_w, L0_xattn_to_v_others_w, L0_xattn_to_k_ip_w, L0_xattn_to_v_ip_w, L0_xattn_to_out_w, L0_xattn_to_out_b, L1_xattn_Wq, L1_xattn_Wk, L1_xattn_Wv, L1_xattn_Wk_ip, L1_xattn_Wv_ip, L1_xattn_Wout, L1_xattn_bout, L2_xattn_Wq, L2_xattn_Wk, L2_xattn_Wv, L2_xattn_Wk_ip, L2_xattn_Wv_ip, L2_xattn_Wo, L2_xattn_bo, L3_xattn_W_q, L3_xattn_W_k, L3_xattn_W_v, L3_xattn_W_k_ip, L3_xattn_W_v_ip, L3_xattn_W_out, L3_xattn_b_out):
    import jax
    import jax.numpy as jnp

    def _L0_xattn_ref(hidden_states, encoder_hidden_states, to_q_w, to_k_w, to_v_w, to_k_object_w, to_v_object_w, to_k_others_w, to_v_others_w, to_k_ip_w, to_v_ip_w, to_out_w, to_out_b):
        import jax, jax.numpy as jnp
        import numpy as np
        B, S, C = (2, 512, 160)
        CA = 256
        HEADS = 20
        HD = C // HEADS
        N_TXT, N_OBJ, N_OTH, N_IP = (77, 4, 4, 16)
        SCALE_OBJ = SCALE_OTH = SCALE_IP = 1.0
        RESCALE = 1.0

        def _heads(x):
            b, l, _ = x.shape
            return x.reshape(b, l, HEADS, HD).transpose(0, 2, 1, 3)

        def _merge(x):
            b, h, l, d = x.shape
            return x.transpose(0, 2, 1, 3).reshape(b, l, h * d)

        def _sdpa(q, k, v):
            scale = 1.0 / np.sqrt(HD).astype(np.float32)
            s = jnp.einsum('bhqd,bhkd->bhqk', q, k) * scale
            p = jax.nn.softmax(s, axis=-1)
            return jnp.einsum('bhqk,bhkd->bhqd', p, v)
        residual = hidden_states
        end = N_TXT
        ehs_txt = encoder_hidden_states[:, :end]
        ehs_obj = encoder_hidden_states[:, end:end + N_OBJ]
        ehs_oth = encoder_hidden_states[:, end + N_OBJ:end + N_OBJ + N_OTH]
        ehs_ip = encoder_hidden_states[:, end + N_OBJ + N_OTH:]
        q = _heads(hidden_states @ to_q_w)
        h_txt = _sdpa(q, _heads(ehs_txt @ to_k_w), _heads(ehs_txt @ to_v_w))
        h_obj = _sdpa(q, _heads(ehs_obj @ to_k_object_w), _heads(ehs_obj @ to_v_object_w))
        h_oth = _sdpa(q, _heads(ehs_oth @ to_k_others_w), _heads(ehs_oth @ to_v_others_w))
        h_ip = _sdpa(q, _heads(ehs_ip @ to_k_ip_w), _heads(ehs_ip @ to_v_ip_w))
        out = _merge(h_txt) + SCALE_OBJ * _merge(h_obj) + SCALE_OTH * _merge(h_oth) + SCALE_IP * _merge(h_ip)
        out = out @ to_out_w + to_out_b
        out = (out + residual) / RESCALE
        return out

    def _L1_xattn_ref(hidden_states, encoder_hidden_states, spatial_mask, Wq, Wk, Wv, Wk_ip, Wv_ip, Wout, bout):
        import jax, jax.numpy as jnp
        import numpy as np
        import math
        HEADS = 20
        NUM_TOKENS = 4
        SEM_SCALE = 0.5
        IP_SCALE = 1.0
        TEXT_LEN = 77

        def _split_heads(x, B, H, D):
            return x.reshape(B, -1, H, D).transpose(0, 2, 1, 3)
        B, S, C = hidden_states.shape
        D = C // HEADS
        scale = 1.0 / math.sqrt(D)
        residual = hidden_states
        text = encoder_hidden_states[:, :TEXT_LEN]
        ip = encoder_hidden_states[:, TEXT_LEN:]
        q = hidden_states @ Wq
        k_text = text @ Wk
        v_text = text @ Wv
        q_h = _split_heads(q, B, HEADS, D)
        k_h = _split_heads(k_text, B, HEADS, D)
        v_h = _split_heads(v_text, B, HEADS, D)
        logits = jnp.einsum('bhqd,bhkd->bhqk', q_h, k_h) * scale
        probs = jax.nn.softmax(logits, axis=-1)
        text_out = jnp.einsum('bhqk,bhkd->bhqd', probs, v_h)
        text_out = text_out.transpose(0, 2, 1, 3).reshape(B, S, C)
        ip_k = ip @ Wk_ip
        ip_v = ip @ Wv_ip
        ip_k_h = _split_heads(ip_k, B, HEADS, D)
        ip_v_h = _split_heads(ip_v, B, HEADS, D)
        scores = jnp.einsum('bhqd,bhkd->bhqk', q_h, ip_k_h) * scale
        text_probs = jax.nn.softmax(jnp.einsum('bqc,bkc->bqk', q, k_text) * scale, axis=-1)
        q_sem = jnp.einsum('bqk,bkc->bqc', text_probs, text)
        sem = jnp.einsum('bqc,bnc->bqn', q_sem, ip) * scale
        sem = jax.lax.stop_gradient(sem)
        fused = scores + SEM_SCALE * sem[:, None, :, :]
        ip_probs = jax.nn.softmax(fused, axis=-1)
        ip_probs = ip_probs * spatial_mask[None, None, :, None]
        ip_out = jnp.einsum('bhqk,bhkd->bhqd', ip_probs, ip_v_h)
        ip_out = ip_out.transpose(0, 2, 1, 3).reshape(B, S, C)
        hs = text_out + IP_SCALE * ip_out
        out = hs @ Wout + bout
        out = out + residual
        return out

    def _L2_xattn_ref(hidden_states, encoder_hidden_states, Wq, Wk, Wv, Wk_ip, Wv_ip, Wo, bo):
        import jax, jax.numpy as jnp
        import numpy as np
        NUM_HEADS = 20
        TEXT_LEN = 77
        IP_SCALE = 1.0

        def _attend(q, k, v, sm_scale):
            scores = jnp.einsum('bhsd,bhld->bhsl', q, k) * sm_scale
            probs = jax.nn.softmax(scores, axis=-1)
            return jnp.einsum('bhsl,bhld->bhsd', probs, v)

        def _split_heads(x, h):
            b, s, c = x.shape
            return x.reshape(b, s, h, c // h).transpose(0, 2, 1, 3)

        def _merge_heads(x):
            b, h, s, d = x.shape
            return x.transpose(0, 2, 1, 3).reshape(b, s, h * d)
        residual = hidden_states
        B, S, C = hidden_states.shape
        H = NUM_HEADS
        D = C // H
        sm_scale = 1.0 / jnp.sqrt(jnp.asarray(D, hidden_states.dtype))
        text = encoder_hidden_states[:, :TEXT_LEN, :]
        ip = encoder_hidden_states[:, TEXT_LEN:, :]
        q = _split_heads(hidden_states @ Wq.T, H)
        k = _split_heads(text @ Wk.T, H)
        v = _split_heads(text @ Wv.T, H)
        out_text = _merge_heads(_attend(q, k, v, sm_scale))
        k_ip = _split_heads(ip @ Wk_ip.T, H)
        v_ip = _split_heads(ip @ Wv_ip.T, H)
        out_ip = _merge_heads(_attend(q, k_ip, v_ip, sm_scale))
        out = out_text + IP_SCALE * out_ip
        out = out @ Wo.T + bo
        return out + residual

    def _L3_xattn_ref(hidden_states, encoder_hidden_states, spatial_mask, W_q, W_k, W_v, W_k_ip, W_v_ip, W_out, b_out):
        import jax, jax.numpy as jnp
        import numpy as np
        HEADS = 20
        NUM_TOKENS = 4
        IP_SCALE = 1.0
        SEM_SCALE = 0.5
        RESCALE = 1.0
        EPS = 1e-12

        def _l2norm(x, axis=-1):
            n = jnp.sqrt(jnp.sum(x * x, axis=axis, keepdims=True))
            return x / jnp.maximum(n, EPS)
        B, S, C = hidden_states.shape
        H = HEADS
        Dh = C // H
        attn_scale = Dh ** (-0.5)
        residual = hidden_states
        text_ehs = encoder_hidden_states[:, :-NUM_TOKENS]
        ip_ehs = encoder_hidden_states[:, -NUM_TOKENS:]

        def heads(x):
            return x.reshape(B, -1, H, Dh).transpose(0, 2, 1, 3)
        q = heads(hidden_states @ W_q)
        k_t = heads(text_ehs @ W_k)
        v_t = heads(text_ehs @ W_v)
        scores_t = jnp.einsum('bhsd,bhtd->bhst', q, k_t) * attn_scale
        probs_t = jax.nn.softmax(scores_t, axis=-1)
        text_out = jnp.einsum('bhst,bhtd->bhsd', probs_t, v_t)
        text_out = text_out.transpose(0, 2, 1, 3).reshape(B, S, C)
        k_ip = heads(ip_ehs @ W_k_ip)
        v_ip = heads(ip_ehs @ W_v_ip)
        attn_scores = jnp.einsum('bhsd,bhnd->bhsn', q, k_ip) * attn_scale
        qsem = jnp.einsum('bhst,bte->bhse', probs_t, text_ehs)
        qsem = _l2norm(qsem)
        ip_n = _l2norm(ip_ehs)
        sem = jnp.einsum('bhse,bne->bhsn', qsem, ip_n)
        sem = jax.lax.stop_gradient(sem)
        fused = attn_scores + SEM_SCALE * sem
        probs_ip = jax.nn.softmax(fused, axis=-1)
        probs_ip = probs_ip * spatial_mask[None, None, :, None]
        ip_out = jnp.einsum('bhsn,bhnd->bhsd', probs_ip, v_ip)
        ip_out = ip_out.transpose(0, 2, 1, 3).reshape(B, S, C)
        out = text_out + IP_SCALE * ip_out
        out = out @ W_out + b_out
        out = out + residual
        return out / RESCALE
    x = _L0_xattn_ref(x, ctx_2048, L0_xattn_to_q_w, L0_xattn_to_k_w, L0_xattn_to_v_w, L0_xattn_to_k_object_w, L0_xattn_to_v_object_w, L0_xattn_to_k_others_w, L0_xattn_to_v_others_w, L0_xattn_to_k_ip_w, L0_xattn_to_v_ip_w, L0_xattn_to_out_w, L0_xattn_to_out_b)
    x = _L1_xattn_ref(x, ctx_2048, fside_S_0, L1_xattn_Wq, L1_xattn_Wk, L1_xattn_Wv, L1_xattn_Wk_ip, L1_xattn_Wv_ip, L1_xattn_Wout, L1_xattn_bout)
    x = _L2_xattn_ref(x, ctx_2048, L2_xattn_Wq, L2_xattn_Wk, L2_xattn_Wv, L2_xattn_Wk_ip, L2_xattn_Wv_ip, L2_xattn_Wo, L2_xattn_bo)
    x = _L3_xattn_ref(x, ctx_2048, fside_S_0, L3_xattn_W_q, L3_xattn_W_k, L3_xattn_W_v, L3_xattn_W_k_ip, L3_xattn_W_v_ip, L3_xattn_W_out, L3_xattn_b_out)
    return x

_drawn_inputs = setup_inputs


def setup_inputs(seed=0):
    import zlib

    import numpy as np

    out = dict(_drawn_inputs(seed))
    spreads = {'L0_xattn_to_out_b': (0.0, 0.1),
     'L1_xattn_bout': (0.0, 0.1),
     'L2_xattn_bo': (0.0, 0.1),
     'L3_xattn_b_out': (0.0, 0.1)}
    factors = {}
    for name, (base, spread) in spreads.items():
        noise = np.random.default_rng([zlib.crc32(name.encode()), seed]).standard_normal(out[name].shape)
        drawn = base * np.exp(spread * noise) if base else spread * noise
        out[name] = jnp.asarray(drawn.astype(out[name].dtype))
    for name, factor in factors.items():
        out[name] = (out[name] * factor).astype(out[name].dtype)
    return out
```

```python
from contextlib import ExitStack

import numpy as np

import concourse.bass as bass
from concourse import mybir

B, S, C = 64, 128, 160
T, E = 77, 256
H, D = 20, 8
L = 4
NIP = 4
TXT = T - NIP
SCALE = float(np.float32(1.0) / np.sqrt(np.float32(D)))

HC = C // 2
HH = H // 2
NB = 4
GROUPS = B // NB
STEPS = L * NB
QH = 5
QC = QH * T

TRI = (H + 2) // 3
FIRST = T + (T + 1) // 2
CUT = FIRST - T
UC = 3 * D + 3
PPAD = 3 * T * (TRI - 1) + FIRST + 128
PCOLS = max(PPAD, H * T)
PWAVES = [(0, range(0, 4)), (1, range(0, 4)), (0, range(4, TRI)), (1, range(4, TRI))]
CX = 128 + 128 + H * NIP

F32 = mybir.dt.float32
ALU = mybir.AluOpType
ACT = mybir.ActivationFunctionType
AX = mybir.AxisListType


def rows_of(kind):
    if kind == 0:
        return [(0, t) for t in range(T)] + [(1, t) for t in range(CUT)]
    return [(1, t) for t in range(CUT, T)] + [(2, t) for t in range(T)]


def heads_of(kind):
    return [tuple(h if h < H else None for h in (3 * g + kind, 3 * g + kind + 1)) for g in range(TRI)]


def build(nc, a):
    ctx = ExitStack()
    with ctx:
        def sb(name, shape):
            return ctx.enter_context(nc.sbuf_tensor(name, shape, F32))

        def pb(name, shape):
            return ctx.enter_context(nc.psum_tensor(name, shape, F32))

        def sem(name):
            return ctx.enter_context(nc.semaphore(name))

        wq = sb("wq", [128, L * 2 * C])
        wo = sb("wo", [128, L * 2 * C])
        wk = sb("wk", [128, L * 2 * C])
        wkip = sb("wkip", [128, 2 * C])
        wv = sb("wv", [128, L * 2 * 2 * TRI * 2 * D])
        wvip = sb("wvip", [128, 2 * C])
        ident = sb("ident", [128, 128])
        ones = sb("ones", [128, 128])
        fside = sb("fside", [128, 1])
        mask_k = sb("mask_k", [HC, HH])
        mask_v = sb("mask_v", [128, 2 * 2 * D])
        mask_g = sb("mask_g", [128, 2 * 2 * T])
        mask_z = sb("mask_z", [128, 2 * 3 * NIP])
        mask_vip = sb("mask_vip", [H * NIP, C])
        nhalf = sb("nhalf", [128, H])

        x_in = [sb(f"x_in{b}", [128, 2 * S]) for b in range(NB)]
        x_work = [sb(f"x_work{b}", [128, 2 * S]) for b in range(NB)]
        x_out = [sb(f"x_out{b}", [HC, 2 * S]) for b in range(NB)]
        context = [sb(f"context{b}", [128, 2 * CX]) for b in range(NB)]
        k_dense = sb("k_dense", [HC, 2 * T])
        k_blocks = [sb(f"k_blocks{i}", [128, 2 * HH * T]) for i in range(2)]
        q_t = [sb(f"q_t{i}", [128, 2 * S]) for i in range(2)]
        v_rows = [sb(f"v_rows{b}", [128, 2 * TRI * UC]) for b in range(NB)]
        top = sb("top", [128, 2 * H])
        probs = [sb(f"probs{i}", [128, PCOLS]) for i in range(2)]
        probs_t = [sb(f"probs_t{i}", [128, 2 * TRI * S]) for i in range(2)]
        u_sb = sb("u_sb", [128, 4 * S])
        recip = sb("recip", [128, 3 * TRI])
        o_sb = sb("o_sb", [128, 3 * TRI * D])
        o_t = sb("o_t", [128, 2 * S])
        ip_sq = sb("ip_sq", [128, 2 * NIP])
        ip_n2 = sb("ip_n2", [128, NIP])
        ip_rn = [sb(f"ip_rn{b}", [128, NIP]) for b in range(NB)]
        gram = [sb(f"gram{b}", [128, 2 * 2 * T]) for b in range(NB)]
        z_rows = [sb(f"z_rows{b}", [128, 2 * 3 * NIP]) for b in range(NB)]
        v_ip = [sb(f"v_ip{b}", [H * NIP, C]) for b in range(NB)]
        s_ip = [sb(f"s_ip{b}", [128, H * NIP]) for b in range(NB)]
        weighted = sb("weighted", [128, H * T])
        q_n2 = [sb(f"q_n2{b}", [128, H]) for b in range(NB)]
        den = sb("den", [128, 3 * TRI])
        den2 = sb("den2", [128, 3 * TRI])
        q_cl = sb("q_cl", [128, H])
        q_rn = sb("q_rn", [128, H])
        z_a = sb("z_a", [128, H * NIP])
        z_b = sb("z_b", [128, H * NIP])
        fused = sb("fused", [128, H * NIP])
        f_top = sb("f_top", [128, H])
        f_sub = sb("f_sub", [128, H * NIP])
        f_exp = sb("f_exp", [128, H * NIP])
        f_sum = sb("f_sum", [128, H])
        f_rec = sb("f_rec", [128, H])
        f_wgt = sb("f_wgt", [128, H])
        p_ip = sb("p_ip", [128, H * NIP])
        p_ip_t = sb("p_ip_t", [H * NIP, S])

        ps_s = pb("ps_s", [128, 4 * 512])
        ps_t = pb("ps_t", [128, 2 * 512])
        ps_c = pb("ps_c", [128, 512])
        ps_p = pb("ps_p", [128, 512])

        def w_half(w, l, kt, lo, n):
            at = (l * 2 + kt) * C + lo
            return w[:, at:at + n]

        def wv_half(l, kind, kt):
            n = TRI * 2 * D
            at = ((l * 2 + kind) * 2 + kt) * n
            return wv[:, at:at + n]

        def cx(b, kt, lo, n):
            return context[b][:, kt * CX + lo:kt * CX + lo + n]

        def chunk(kind, g):
            at = 3 * T * g + FIRST * kind
            return at, (kind * TRI + g) * S

        ld_w = sem("ld_w")
        ld_x = [sem(f"ld_x{b}") for b in range(NB)]
        ld_c = [sem(f"ld_c{b}") for b in range(NB)]
        st_x = [sem(f"st_x{b}") for b in range(NB)]
        setup = sem("setup")
        setup_pool = sem("setup_pool")
        k_psum = sem("k_psum")
        k_evac = sem("k_evac")
        k_ready = sem("k_ready")
        v_psum = sem("v_psum")
        v_ready = sem("v_ready")
        g_psum = sem("g_psum")
        g_ready = sem("g_ready")
        sq_ready = sem("sq_ready")
        n2_ready = sem("n2_ready")
        rn_ready = sem("rn_ready")
        q_psum = sem("q_psum")
        q_evac = sem("q_evac")
        s_psum = sem("s_psum")
        s_top = sem("s_top")
        s_sub = sem("s_sub")
        p_ready = sem("p_ready")
        t_psum = sem("t_psum")
        t_evac = sem("t_evac")
        u_psum = sem("u_psum")
        u_evac = sem("u_evac")
        ut_psum = sem("ut_psum")
        r_ready = sem("r_ready")
        o_ready = sem("o_ready")
        ot_psum = sem("ot_psum")
        ot_evac = sem("ot_evac")
        y_psum = sem("y_psum")
        x_ready = sem("x_ready")
        w_psum = sem("w_psum")
        w_ready = sem("w_ready")
        qn_ready = sem("qn_ready")
        ip_step = sem("ip_step")
        cl_ready = sem("cl_ready")
        qrn_ready = sem("qrn_ready")
        f_ready = sem("f_ready")
        fe_ready = sem("fe_ready")
        pip_ready = sem("pip_ready")
        pipt_psum = sem("pipt_psum")
        pipt_evac = sem("pipt_evac")

        block = ctx.enter_context(nc.Block())

        def wait(eng, s, k, c, per=1, more=0):
            n = per * c + more
            if isinstance(k, int):
                n += per * STEPS * k
                if n <= 0:
                    return
                eng.wait_ge(s, n)
            else:
                assert n >= 0
                eng.wait_ge(s, k * (per * STEPS) + n)

        def wait_last(eng, s, k, c, per=1, more=0):
            n = per * (NB * (c // STEPS) + max(0, c % STEPS - (STEPS - NB))) + more
            if isinstance(k, int):
                n += per * NB * k
                if n <= 0:
                    return
                eng.wait_ge(s, n)
            else:
                assert n >= 0
                eng.wait_ge(s, k * (per * NB) + n)

        def layer(c):
            return c % STEPS // NB

        def last(c):
            return layer(c) == L - 1

        def run(eng, step):
            step(0, 0)
            step(0, 1)
            with eng.Fori(0, GROUPS - 1) as k:
                for j in range(STEPS):
                    step(k, j + 2)
            for j in range(2, STEPS + 2):
                step(GROUPS - 1, j)

        def exists(k, c):
            if isinstance(k, int):
                return 0 <= STEPS * k + c < STEPS * GROUPS
            return True

        WEIGHTS = [(wq[0:HC, :], a["wq"]), (wo[0:HC, :], a["wo"]), (wk[:, :], a["wk"]),
                   (wkip[:, :], a["wkip"]), (wv[:, :], a["wv"]), (wvip[:, :], a["wvip"]),
                   (ident[:, :], a["ident"]), (fside[:, :], a["fside"]), (mask_k[:, :], a["mask_k"]),
                   (mask_v[:, :], a["mask_v"]), (mask_g[:, :], a["mask_g"]),
                   (mask_z[:, :], a["mask_z"]), (mask_vip[:, :], a["mask_vip"])]
        N_SET, N_SET_POOL = 17, 5
        N_LD = 16 * (len(WEIGHTS) + 1 + NB)

        @block.sync
        def _(sp):
            sp.wait_ge(setup, N_SET)
            for b in range(NB):
                sp.dma_start(context[b][:, :], a["ctx"][b, :, :]).then_inc(ld_c[b], 16)
                sp.dma_start(x_in[b][0:HC, :], a["x"][b, :, :]).then_inc(ld_x[b], 16)
            with sp.Fori(0, GROUPS - 1) as k:
                for b in range(NB):
                    wait(sp, x_ready, k, b + 1)
                    sp.dma_start(x_in[b][0:HC, :],
                                 a["x"][bass.ds(k * NB + (NB + b), 1), :, :].rearrange("a p n -> (a p) n"))\
                        .then_inc(ld_x[b], 16)
                for b in range(NB):
                    wait_last(sp, g_psum, k, STEPS - NB + b + 1)
                    sp.dma_start(context[b][:, :],
                                 a["ctx"][bass.ds(k * NB + (NB + b), 1), :, :].rearrange("a p n -> (a p) n"))\
                        .then_inc(ld_c[b], 16)
                for b in range(NB):
                    wait(sp, x_ready, k, STEPS - NB + b + 1)
                    sp.dma_start(a["out"][bass.ds(k * NB + b, 1), :, :].rearrange("a p n -> (a p) n"),
                                 x_out[b][:, :]).then_inc(st_x[b], 16)
            for b in range(NB):
                wait(sp, x_ready, GROUPS - 1, STEPS - NB + b + 1)
                sp.dma_start(a["out"][(GROUPS - 1) * NB + b, :, :], x_out[b][:, :]).then_inc(st_x[b], 16)
            for b in range(NB):
                sp.wait_ge(st_x[b], 16 * GROUPS)

        @block.tensor
        def _(pe):
            def keys(k, c):
                l, b = layer(c), c % NB
                if l == 0:
                    pe.wait_ge(ld_c[b], (k + c // STEPS) * 16 + 16)
                wait(pe, q_evac, k, c)
                n = TXT if last(c) else T
                for m in range(2):
                    for kt in range(2):
                        ins = pe.matmul(ps_p[0:HC, m * T:m * T + n], w_half(wk, l, kt, m * HC, HC),
                                        cx(b, kt, 0, n), start=kt == 0, stop=kt == 1)
                    if last(c):
                        for kt in range(2):
                            ins = pe.matmul(ps_p[0:HC, m * T + n:(m + 1) * T], w_half(wkip, 0, kt, m * HC, HC),
                                            cx(b, kt, n, NIP), start=kt == 0, stop=kt == 1)
                ins.then_inc(k_psum, 1)

            def values(k, c):
                l, b = layer(c), c % NB
                wait(pe, k_evac, k, c + 1)
                n = TRI * 2 * D
                for kind in range(2):
                    for kt in range(2):
                        ins = pe.matmul(ps_p[:, kind * n:kind * n + n], cx(b, kt, kind * 128, 128),
                                        wv_half(l, kind, kt), start=kt == 0, stop=kt == 1)
                ins.then_inc(v_psum, 1)

            def image(k, c):
                b = c % NB
                wait(pe, v_ready, k, c + 1)
                for kind in range(2):
                    for at, lo, n in ((kind * T, 0, T), (2 * T + kind * NIP, TXT, NIP)):
                        for kt in range(2):
                            pe.matmul(ps_p[:, at:at + n], cx(b, kt, kind * 128, 128), cx(b, kt, lo, n),
                                      start=kt == 0, stop=kt == 1)
                wait_last(pe, sq_ready, k, c + 1)
                at = 2 * T + 2 * NIP
                for kt in range(2):
                    pe.matmul(ps_p[:, at:at + NIP], ones[:, :], ip_sq[:, kt * NIP:(kt + 1) * NIP],
                              start=kt == 0, stop=kt == 1)
                at += NIP + 2
                for kt in range(2):
                    ins = pe.matmul(ps_p[0:H * NIP, at:at + C], cx(b, kt, 256, H * NIP),
                                    wvip[:, kt * C:(kt + 1) * C], start=kt == 0, stop=kt == 1)
                ins.then_inc(g_psum, 1)

            def queries(k, c):
                l, b = layer(c), c % NB
                if last(c):
                    wait_last(pe, g_ready, k, c + 1)
                else:
                    wait(pe, v_ready, k, c + 1)
                if l == 0:
                    pe.wait_ge(ld_x[b], (k + c // STEPS) * 16 + 16)
                else:
                    wait(pe, x_ready, k, c - NB + 1)
                x = x_in[b] if l == 0 else x_work[b]
                for m in range(2):
                    for kt in range(2):
                        ins = pe.matmul(ps_p[0:HC, m * S:(m + 1) * S], w_half(wq, l, kt, m * HC, HC),
                                        x[:, kt * S:(kt + 1) * S], start=kt == 0, stop=kt == 1)
                ins.then_inc(q_psum, 1)

            def scores(k, c, q):
                m = q // 2
                if q == 0:
                    wait(pe, q_evac, k, c + 1)
                if q % 2 == 0:
                    wait(pe, k_ready, k, c, per=2, more=m + 1)
                wait(pe, s_sub, k, c - 1, per=4, more=q + 1)
                if last(c - 2) and exists(k, c - 2):
                    wait_last(pe, w_ready, k, c - 2, per=4, more=q + 1)
                at = q * QC
                pe.matmul(ps_s[:, q * 512:q * 512 + QC], q_t[c % 2][:, m * S:(m + 1) * S],
                          k_blocks[c % 2][:, at:at + QC], start=True, stop=True).then_inc(s_psum, 1)

            def turn(k, c, w):
                kind, gs = PWAVES[w]
                if w == 0:
                    wait(pe, p_ready, k, c + 1, per=4)
                wait(pe, t_evac, k, c, per=4, more=w - 1)
                for i, g in enumerate(gs):
                    at, _ = chunk(kind, g)
                    to = (w % 2) * 512 + i * S
                    ins = pe.transpose(ps_t[:, to:to + S], probs[c % 2][:, at:at + 128], ident[:, :])
                ins.then_inc(t_psum, 1)

            def product(k, c, w):
                kind, gs = PWAVES[w]
                b = c % NB
                if w == 0:
                    wait(pe, v_ready, k, c + 1)
                    wait(pe, x_ready, k, c)
                wait(pe, t_evac, k, c, per=4, more=w + 1)
                for g in gs:
                    _, at = chunk(kind, g)
                    ins = pe.matmul(ps_c[32 * (g % 4):32 * (g % 4) + UC, g // 4 * S:(g // 4 + 1) * S],
                                    v_rows[b][:, (kind * TRI + g) * UC:(kind * TRI + g + 1) * UC],
                                    probs_t[c % 2][:, at:at + S], start=kind == 0, stop=kind == 1)
                if last(c) and kind == 1:
                    if w == 1:
                        wait_last(pe, g_ready, k, c + 1)
                    n = 3 * NIP
                    for kd in range(2):
                        for g in gs:
                            _, at = chunk(kd, g)
                            ins = pe.matmul(ps_c[32 * (g % 4):32 * (g % 4) + n,
                                                 (2 + g // 4) * S:(3 + g // 4) * S],
                                            z_rows[b][:, kd * n:(kd + 1) * n],
                                            probs_t[c % 2][:, at:at + S], start=kd == 0, stop=kd == 1)
                if w == 3:
                    ins.then_inc(u_psum, 1)

            def gram_product(k, c):
                b = c % NB
                for z in range(4):
                    if exists(k, c + 1):
                        wait(pe, s_sub, k, c + 1, per=4, more=z + 1)
                    else:
                        wait(pe, s_sub, k, c, per=4, more=z + 1)
                    for g in range(2 * z, min(2 * z + 2, TRI)):
                        for kind in range(2):
                            _, at = chunk(kind, g)
                            to = z * 512 + (g % 2) * 3 * T + kind * T
                            ins = pe.matmul(ps_s[:, to:to + 2 * T], probs_t[c % 2][:, at:at + S],
                                            gram[b][:, kind * 2 * T:(kind + 1) * 2 * T],
                                            start=g % 2 == 0 and kind == 0, stop=kind == 1,
                                            skip_group_check=True)
                    ins.then_inc(w_psum, 1)

            def turn_back(k, c):
                wait(pe, u_evac, k, c + 1)
                for i in range(4 if last(c) else 2):
                    ins = pe.transpose(ps_c[:, i * S:(i + 1) * S], u_sb[:, i * S:(i + 1) * S], ident[:, :])
                ins.then_inc(ut_psum, 1)

            def turn_out(k, c):
                b = c % NB
                wait(pe, o_ready, k, c + 1)
                if last(c):
                    wait_last(pe, pip_ready, k, c + 1)
                    pe.transpose(ps_c[0:H * NIP, 2 * S:3 * S], p_ip[:, :], ident[:, :]).then_inc(pipt_psum, 1)
                    wait_last(pe, pipt_evac, k, c + 1)
                for m in range(2):
                    ins = pe.matmul(ps_c[0:HC, m * S:(m + 1) * S], o_sb[:, m * HC:(m + 1) * HC], ident[:, :],
                                    is_transpose=True, start=True, stop=not last(c))
                    if last(c):
                        ins = pe.matmul(ps_c[0:HC, m * S:(m + 1) * S], v_ip[b][:, m * HC:(m + 1) * HC],
                                        p_ip_t[:, :], start=False, stop=True)
                ins.then_inc(ot_psum, 1)

            def project_out(k, c):
                l = layer(c)
                wait(pe, ot_evac, k, c + 1)
                for m in range(2):
                    for kt in range(2):
                        ins = pe.matmul(ps_c[0:HC, m * S:(m + 1) * S], w_half(wo, l, kt, m * HC, HC),
                                        o_t[:, kt * S:(kt + 1) * S], start=kt == 0, stop=kt == 1)
                ins.then_inc(y_psum, 1)

            def step(k, c):
                now, prev, out, nxt = exists(k, c), exists(k, c - 1), exists(k, c - 2), exists(k, c + 1)
                if now:
                    scores(k, c, 0)
                if out:
                    turn_back(k, c - 2)
                if now:
                    scores(k, c, 1)
                    scores(k, c, 2)
                if out:
                    turn_out(k, c - 2)
                if now:
                    scores(k, c, 3)
                if prev:
                    turn(k, c - 1, 0)
                    turn(k, c - 1, 1)
                if out:
                    project_out(k, c - 2)
                if nxt:
                    keys(k, c + 1)
                if prev:
                    product(k, c - 1, 0)
                    turn(k, c - 1, 2)
                if nxt:
                    values(k, c + 1)
                if prev:
                    product(k, c - 1, 1)
                    turn(k, c - 1, 3)
                if nxt and last(c + 1):
                    image(k, c + 1)
                if prev:
                    product(k, c - 1, 2)
                if nxt:
                    queries(k, c + 1)
                if prev:
                    product(k, c - 1, 3)
                    if last(c - 1):
                        gram_product(k, c - 1)

            pe.wait_ge(ld_w, N_LD)
            pe.wait_ge(setup, N_SET)
            pe.wait_ge(setup_pool, N_SET_POOL)
            keys(0, 0)
            values(0, 0)
            queries(0, 0)
            run(pe, step)

        @block.scalar
        def _(act):
            act.wait_ge(setup, N_SET)
            for n, (tile, src) in enumerate(WEIGHTS):
                act.dma_start(tile, src).then_inc(ld_w, 16)
            act.dma_start(wo[96:97, :], a["bias"]).then_inc(ld_w, 16)
            for b in range(NB):
                act.dma_start(v_rows[b][:, :], a["v_fixed"]).then_inc(ld_w, 16)
            act.wait_ge(ld_w, N_LD)

            def keys(k, c):
                wait(act, k_psum, k, c + 1)
                wait(act, k_ready, k, c, per=2)
                act.activation(k_dense[:, :], ps_p[0:HC, 0:2 * T], ACT.Copy).then_inc(k_evac, 1)

            def queries(k, c):
                wait(act, q_psum, k, c + 1)
                wait(act, s_psum, k, c - 1, per=4)
                act.activation(q_t[c % 2][0:HC, :], ps_p[0:HC, 0:2 * S], ACT.Copy).then_inc(q_evac, 1)

            def exps(k, c, q):
                wait(act, s_sub, k, c, per=4, more=q + 1)
                n = TXT if last(c) else T
                p = probs[c % 2][:, q * QC:(q + 1) * QC].rearrange("p (h t) -> p h t", t=T)[:, :, 0:n]
                act.activation(p, p, ACT.Exp, scale=SCALE).then_inc(p_ready, 1)

            def turned(k, c, w):
                kind, gs = PWAVES[w]
                wait(act, t_psum, k, c, per=4, more=w + 1)
                if w == 0:
                    wait(act, u_psum, k, c - 1)
                    if last(c - 2) and exists(k, c - 2):
                        wait_last(act, w_psum, k, c - 1, per=4)
                _, at = chunk(kind, gs[0])
                n = len(gs) * S
                act.activation(probs_t[c % 2][:, at:at + n], ps_t[:, (w % 2) * 512:(w % 2) * 512 + n],
                               ACT.Copy).then_inc(t_evac, 1)

            def products(k, c):
                wait(act, u_psum, k, c + 1)
                wait(act, ut_psum, k, c)
                n = (4 if last(c) else 2) * S
                act.activation(u_sb[:, 0:n], ps_c[:, 0:n], ACT.Copy).then_inc(u_evac, 1)

            def image_exp(k, c):
                wait_last(act, f_ready, k, c + 1)
                act.activation(f_exp[:, :], f_sub[:, :], ACT.Exp, scale=0.5).then_inc(fe_ready, 1)

            def results(k, c):
                if last(c):
                    wait_last(act, pipt_psum, k, c + 1)
                    act.activation(p_ip_t[:, :], ps_c[0:H * NIP, 2 * S:3 * S], ACT.Copy).then_inc(pipt_evac, 1)
                wait(act, ot_psum, k, c + 1)
                wait(act, y_psum, k, c)
                act.activation(o_t[0:HC, :], ps_c[0:HC, 0:2 * S], ACT.Copy).then_inc(ot_evac, 1)

            def step(k, c):
                now, prev, out, nxt = exists(k, c), exists(k, c - 1), exists(k, c - 2), exists(k, c + 1)
                if out:
                    products(k, c - 2)
                    if last(c - 2):
                        image_exp(k, c - 2)
                if now:
                    exps(k, c, 0)
                    exps(k, c, 1)
                if out:
                    results(k, c - 2)
                if prev:
                    turned(k, c - 1, 0)
                    turned(k, c - 1, 1)
                if nxt:
                    keys(k, c + 1)
                if now:
                    exps(k, c, 2)
                if prev:
                    turned(k, c - 1, 2)
                    turned(k, c - 1, 3)
                if now:
                    exps(k, c, 3)
                if nxt:
                    queries(k, c + 1)

            keys(0, 0)
            queries(0, 0)
            run(act, step)

        @block.vector
        def _(dve):
            zeros = [wq, wo, o_t, u_sb] + x_in + x_work + q_t
            sets = 0
            for tile in zeros:
                dve.memset(tile[:, :], 0.0).then_inc(setup, 1)
                sets += 1
            dve.memset(ps_c[:, :], 0.0).then_inc(setup, 1)
            dve.wait_ge(setup, sets + 1)
            dve.memset(o_t[96:97, 0:S], 1.0).then_inc(setup, 1)
            dve.memset(ones[:, :], 1.0).then_inc(setup, 1)
            assert sets + 3 == N_SET
            dve.wait_ge(setup_pool, N_SET_POOL)
            dve.wait_ge(ld_w, N_LD)

            def top_of(k, c, q):
                wait(dve, s_psum, k, c, per=4, more=q + 1)
                n = TXT if last(c) else T
                s = ps_s[:, q * 512:q * 512 + QC].rearrange("p (h t) -> p h t", t=T)
                at = (c % 2) * H + q * QH
                dve.tensor_reduce(top[:, at:at + QH], s[:, :, 0:n], AX.X, ALU.max).then_inc(s_top, 1)

            def less_top(k, c, q):
                n = TXT if last(c) else T
                s = ps_s[:, q * 512:q * 512 + QC].rearrange("p (h t) -> p h t", t=T)
                p = probs[c % 2][:, q * QC:(q + 1) * QC].rearrange("p (h t) -> p h t", t=T)
                at = (c % 2) * H + q * QH
                if q == 0:
                    wait(dve, t_psum, k, c - 1, per=4)
                if last(c):
                    dve.tensor_copy(s_ip[c % NB][:, q * QH * NIP:(q + 1) * QH * NIP]
                                    .rearrange("p (h t) -> p h t", t=NIP), s[:, :, n:T])
                    dve.memset(p[:, :, n:T], 0.0)
                wait(dve, s_top, k, c, per=4, more=q + 1)
                dve.tensor_tensor(p[:, :, 0:n], s[:, :, 0:n],
                                  top[:, at:at + QH].unsqueeze(2).to_broadcast([128, QH, n]),
                                  ALU.subtract).then_inc(s_sub, 1)

            def values(k, c):
                b = c % NB
                wait(dve, v_psum, k, c + 1)
                wait(dve, u_psum, k, c - NB + 1)
                n = TRI * 2 * D
                for kind in range(2):
                    v = v_rows[b][:, kind * TRI * UC:(kind + 1) * TRI * UC].rearrange("p (g u) -> p g u", u=UC)
                    m = mask_v[:, kind * 2 * D:(kind + 1) * 2 * D].unsqueeze(1).to_broadcast([128, TRI, 2 * D])
                    ins = dve.tensor_tensor(v[:, :, kind * D:kind * D + 2 * D],
                                            ps_p[:, kind * n:(kind + 1) * n].rearrange("p (g u) -> p g u", g=TRI),
                                            m, ALU.mult)
                ins.then_inc(v_ready, 1)

            def image_squares(k, c):
                b = c % NB
                wait_last(dve, g_psum, k, c)
                s = context[b][:, :].rearrange("p (a n) -> p a n", a=2)[:, :, TXT:T]
                dve.tensor_tensor(ip_sq[:, :].rearrange("p (a n) -> p a n", a=2), s, s, ALU.mult)\
                   .then_inc(sq_ready, 1)

            def image(k, c):
                b = c % NB
                wait_last(dve, g_psum, k, c + 1)
                wait_last(dve, rn_ready, k, c)
                at = 2 * T + 2 * NIP
                dve.tensor_scalar(ip_n2[:, :], ps_p[:, at:at + NIP], 1e-24, None, ALU.max).then_inc(n2_ready, 1)
                at += NIP + 2
                dve.tensor_tensor(v_ip[b][:, :], ps_p[0:H * NIP, at:at + C], mask_vip[:, :], ALU.mult)
                for kind in range(2):
                    dve.tensor_tensor(gram[b][:, kind * 2 * T:(kind + 1) * 2 * T].rearrange("p (h t) -> p h t", t=T),
                                      ps_p[:, kind * T:(kind + 1) * T].unsqueeze(1).to_broadcast([128, 2, T]),
                                      mask_g[:, kind * 2 * T:(kind + 1) * 2 * T].rearrange("p (h t) -> p h t", t=T),
                                      ALU.mult)
                    n = 3 * NIP
                    z = 2 * T + kind * NIP
                    ins = dve.tensor_tensor(z_rows[b][:, kind * n:(kind + 1) * n].rearrange("p (h t) -> p h t", t=NIP),
                                            ps_p[:, z:z + NIP].unsqueeze(1).to_broadcast([128, 3, NIP]),
                                            mask_z[:, kind * n:(kind + 1) * n].rearrange("p (h t) -> p h t", t=NIP),
                                            ALU.mult)
                ins.then_inc(g_ready, 1)

            def norms(k, c):
                for z in range(4):
                    lo, hi = 6 * z, min(6 * z + 6, H)
                    wait_last(dve, w_psum, k, c, per=4, more=z + 1)
                    dve.tensor_tensor(weighted[:, lo * T:hi * T], ps_s[:, z * 512:z * 512 + (hi - lo) * T],
                                      probs[c % 2][:, lo * T:hi * T], ALU.mult).then_inc(w_ready, 1)
                wait_last(dve, w_ready, k, c + 1, per=4)
                dve.tensor_reduce(q_n2[c % NB][:, :], weighted[:, :].rearrange("p (h t) -> p h t", t=T),
                                  AX.X, ALU.add).then_inc(qn_ready, 1)

            def by_triple(ap, n):
                return ap.rearrange("p (g x) -> p g x", g=TRI)

            def results(k, c):
                u = ps_c[:, 0:TRI * 32].rearrange("p (g x) -> p g x", x=32)
                wait(dve, ut_psum, k, c + 1)
                dve.reciprocal(recip[:, :].rearrange("p (g i) -> p g i", i=3), u[:, :, 3 * D:3 * D + 3])\
                   .then_inc(r_ready, 1)
                if last(c):
                    dve.tensor_copy(den[:, :].rearrange("p (g i) -> p g i", i=3), u[:, :, 3 * D:3 * D + 3])\
                       .then_inc(ip_step, 1)
                wait(dve, r_ready, k, c + 1)
                wait(dve, ot_psum, k, c)
                ins = dve.tensor_tensor(o_sb[:, :].rearrange("p (g i d) -> p g i d", i=3, d=D),
                                        u[:, :, 0:3 * D].rearrange("p g (i d) -> p g i d", d=D),
                                        recip[:, :].rearrange("p (g i) -> p g i", i=3).unsqueeze(3)
                                        .to_broadcast([128, TRI, 3, D]), ALU.mult)
                ins.then_inc(o_ready, 1)

            IP_STEPS = 10

            def image_branch(k, c):
                b = c % NB
                n_ip = H * NIP

                def per_head(ap):
                    return ap[:, 0:H].unsqueeze(2).to_broadcast([128, H, NIP])

                def per_token(ap):
                    return ap[:, :].rearrange("p (h t) -> p h t", t=NIP)

                def link(ins, n):
                    ins.then_inc(ip_step, 1)
                    wait_last(dve, ip_step, k, c, per=IP_STEPS, more=n)

                wait_last(dve, ip_step, k, c, per=IP_STEPS, more=1)
                link(dve.scalar_tensor_tensor(out=den2[:, :], in0=den[:, :], scalar=1e-24, in1=den[:, :],
                                              op0=ALU.mult, op1=ALU.mult), 2)
                wait_last(dve, qn_ready, k, c + 1)
                dve.tensor_tensor(q_cl[:, :], q_n2[b][:, :], den2[:, 0:H], ALU.max).then_inc(cl_ready, 1)
                z = ps_c[:, 2 * S:2 * S + TRI * 32].rearrange("p (g x) -> p g x", x=32)[:, :, 0:3 * NIP]
                full = TRI - 1
                rn = ip_rn[b][:, :].unsqueeze(1)
                wait_last(dve, rn_ready, k, c + 1)
                dve.tensor_tensor(z_a[:, 0:full * 3 * NIP].rearrange("p (g i t) -> p g i t", i=3, t=NIP),
                                  z[:, 0:full, :].rearrange("p g (i t) -> p g i t", t=NIP),
                                  rn.unsqueeze(1).to_broadcast([128, full, 3, NIP]), ALU.mult)
                link(dve.tensor_tensor(z_a[:, full * 3 * NIP:n_ip].rearrange("p (i t) -> p i t", t=NIP),
                                       z[:, full, 0:(H - 3 * full) * NIP].rearrange("p (i t) -> p i t", t=NIP),
                                       rn.to_broadcast([128, H - 3 * full, NIP]), ALU.mult), 3)
                wait_last(dve, qrn_ready, k, c + 1)
                link(dve.tensor_tensor(per_token(z_b), per_token(z_a), per_head(q_rn), ALU.mult), 4)
                link(dve.scalar_tensor_tensor(out=fused[:, :], in0=s_ip[b][:, :], scalar=2.0 * SCALE, in1=z_b[:, :],
                                              op0=ALU.mult, op1=ALU.add), 5)
                link(dve.tensor_reduce(f_top[:, :], per_token(fused), AX.X, ALU.max), 6)
                dve.tensor_tensor(per_token(f_sub), per_token(fused), per_head(f_top), ALU.subtract)\
                   .then_inc(f_ready, 1)
                wait_last(dve, fe_ready, k, c + 1)
                link(dve.tensor_reduce(f_sum[:, :], per_token(f_exp), AX.X, ALU.add), 7)
                link(dve.reciprocal(f_rec[:, :], f_sum[:, :]), 8)
                link(dve.tensor_scalar(f_wgt[:, :], f_rec[:, :], fside[:, 0:1], None, ALU.mult), 9)
                dve.tensor_tensor(per_token(p_ip), per_token(f_exp), per_head(f_wgt), ALU.mult)\
                   .then_inc(pip_ready, 1)
                dve.tensor_copy(den2[:, 0:1], den[:, 0:1]).then_inc(ip_step, 1)

            def new_x(k, c):
                l, b = layer(c), c % NB
                wait(dve, y_psum, k, c + 1)
                old = x_in[b] if l == 0 else x_work[b]
                to = x_out[b] if l == L - 1 else x_work[b]
                if l == L - 1:
                    n = c // STEPS * 16
                    if isinstance(k, int):
                        n += k * 16
                        if n > 0:
                            dve.wait_ge(st_x[b], n)
                    else:
                        dve.wait_ge(st_x[b], k * 16 + n)
                dve.tensor_tensor(to[0:HC, :], ps_c[0:HC, 0:2 * S], old[0:HC, :], ALU.add).then_inc(x_ready, 1)

            def step(k, c):
                now, prev, out, nxt = exists(k, c), exists(k, c - 1), exists(k, c - 2), exists(k, c + 1)
                if out:
                    results(k, c - 2)
                    if last(c - 2):
                        image_branch(k, c - 2)
                if now:
                    top_of(k, c, 0)
                    top_of(k, c, 1)
                    less_top(k, c, 0)
                    less_top(k, c, 1)
                if out:
                    new_x(k, c - 2)
                if nxt and last(c + 1):
                    image_squares(k, c + 1)
                if now:
                    top_of(k, c, 2)
                    top_of(k, c, 3)
                    less_top(k, c, 2)
                if nxt:
                    values(k, c + 1)
                if now:
                    less_top(k, c, 3)
                if nxt and last(c + 1):
                    image(k, c + 1)
                if prev and last(c - 1):
                    norms(k, c - 1)

            values(0, 0)
            run(dve, step)

        @block.gpsimd
        def _(pool):
            for n in range(2):
                pool.memset(k_blocks[n][:, :], 0.0).then_inc(setup_pool, 1)
                pool.memset(probs[n][:, :], 0.0).then_inc(setup_pool, 1)
            pool.memset(nhalf[:, :], -0.5).then_inc(setup_pool, 1)
            pool.wait_ge(setup_pool, N_SET_POOL)
            pool.wait_ge(ld_w, N_LD)

            def keys(k, c):
                wait(pool, k_evac, k, c + 1)
                wait(pool, s_psum, k, c - 1, per=4)
                for m in range(2):
                    pool.tensor_tensor(k_blocks[c % 2][0:HC, m * HH * T:(m + 1) * HH * T]
                                       .rearrange("p (h t) -> p h t", t=T),
                                       k_dense[:, m * T:(m + 1) * T].unsqueeze(1).to_broadcast([HC, HH, T]),
                                       mask_k[:, :].unsqueeze(2).to_broadcast([HC, HH, T]),
                                       ALU.mult).then_inc(k_ready, 1)

            def step(k, c):
                if exists(k, c - 2) and last(c - 2):
                    wait_last(pool, cl_ready, k, c - 1)
                    pool.tensor_tensor(q_rn[:, :], q_cl[:, :], nhalf[:, :], ALU.pow).then_inc(qrn_ready, 1)
                if exists(k, c + 1):
                    keys(k, c + 1)
                    if last(c + 1):
                        wait_last(pool, n2_ready, k, c + 2)
                        pool.tensor_tensor(ip_rn[(c + 1) % NB][:, :], ip_n2[:, :], nhalf[:, 0:NIP], ALU.pow)\
                            .then_inc(rn_ready, 1)

            keys(0, 0)
            run(pool, step)



def _halves(w, rows):
    return w.reshape(2, rows, w.shape[-1]).transpose(1, 0, 2)


def _layout(inputs):
    f = {k: np.asarray(v) for k, v in inputs.items()}
    n = {"q": ["L0_xattn_to_q_w", "L1_xattn_Wq", "L2_xattn_Wq", "L3_xattn_W_q"],
         "k": ["L0_xattn_to_k_w", "L1_xattn_Wk", "L2_xattn_Wk", "L3_xattn_W_k"],
         "v": ["L0_xattn_to_v_w", "L1_xattn_Wv", "L2_xattn_Wv", "L3_xattn_W_v"],
         "o": ["L0_xattn_to_out_w", "L1_xattn_Wout", "L2_xattn_Wo", "L3_xattn_W_out"],
         "b": ["L0_xattn_to_out_b", "L1_xattn_bout", "L2_xattn_bo", "L3_xattn_b_out"]}

    def weights(kind):
        return [f[name].T if l == 2 else f[name] for l, name in enumerate(n[kind])]

    out = {}
    x = f["x"]
    dt = x.dtype
    out["x"] = x.reshape(B, S, 2, HC).transpose(0, 3, 2, 1).reshape(B, HC, 2 * S)
    ct = f["ctx_2048"].reshape(B, T, 2, 128).transpose(0, 3, 2, 1)
    cx = np.zeros((B, 128, 2, CX), dt)
    for kind in range(2):
        toks = [t for _, t in rows_of(kind)]
        cx[:, :, :, kind * 128:kind * 128 + len(toks)] = ct[:, :, :, toks]
    cx[:, :, :, 256:] = ct[:, :, :, [TXT + i % NIP for i in range(H * NIP)]]
    out["ctx"] = cx.reshape(B, 128, 2 * CX)
    out["wq"] = np.stack([_halves(w, HC) for w in weights("q")], 1).reshape(HC, -1)
    out["wo"] = np.stack([_halves(w, HC) for w in weights("o")], 1).reshape(HC, -1)
    out["wk"] = np.stack([_halves(w, 128) for w in weights("k")], 1).reshape(128, -1)
    out["wkip"] = _halves(f["L3_xattn_W_k_ip"], 128).reshape(128, -1)
    out["wvip"] = _halves(f["L3_xattn_W_v_ip"], 128).reshape(128, -1)
    wv = np.zeros((128, L, 2, 2, TRI, 2, D), dt)
    for l, w in enumerate(weights("v")):
        w = _halves(w, 128).reshape(128, 2, H, D)
        for kind in range(2):
            for g, pair in enumerate(heads_of(kind)):
                for i, h in enumerate(pair):
                    if h is not None:
                        wv[:, l, kind, :, g, i] = w[:, :, h]
    out["wv"] = wv.reshape(128, -1)
    bias = np.zeros((1, L, 2, C), dt)
    for l, name in enumerate(n["b"]):
        bias[0, l, 0] = f[name]
    out["bias"] = bias.reshape(1, -1)
    out["fside"] = f["fside_S_0"].reshape(S, 1)
    out["ident"] = np.eye(128, dtype=dt)
    out["mask_k"] = np.kron(np.eye(HH, dtype=dt), np.ones((D, 1), dt))
    out["mask_vip"] = np.kron(np.eye(H, dtype=dt), np.ones((NIP, D), dt))
    mv = np.zeros((128, 2, 2, D), dt)
    mg = np.zeros((128, 2, 2, T), dt)
    mz = np.zeros((128, 2, 3, NIP), dt)
    vf = np.zeros((128, 2, TRI, UC), dt)
    for kind in range(2):
        for r, (h, t) in enumerate(rows_of(kind)):
            mv[r, kind, h - kind] = 1
            if t < TXT:
                mg[r, kind, h - kind, :TXT] = 1
                mz[r, kind, h] = 1
            vf[r, kind, :, 3 * D + h] = 1
            if h == 1:
                vf[r, kind, TRI - 1, 3 * D + 2] = 1
    out["mask_v"], out["mask_g"], out["mask_z"] = (m.reshape(128, -1) for m in (mv, mg, mz))
    out["v_fixed"] = vf.reshape(128, -1)
    return {k: np.ascontiguousarray(v) for k, v in out.items()}


def kernel(**inputs):
    import concourse.bacc as bacc
    from concourse.bass_utils import run_bass_kernel_spmd

    nc = bacc.Bacc("TRN2", target_bir_lowering=False, num_devices=1)
    arrays, tensors = {}, {}
    for name, v in _layout(inputs).items():
        arrays[f"in_{name}"] = v
        tensors[name] = nc.dram_tensor(f"in_{name}", v.shape, mybir.dt.from_np(v.dtype), kind="ExternalInput").ap()
    tensors["out"] = nc.dram_tensor("out_x", (B, HC, 2 * S), F32, kind="ExternalOutput").ap()
    build(nc, tensors)
    r = run_bass_kernel_spmd(nc, [arrays], core_ids=[0])
    got = np.asarray(r.results[0]["out_x"])
    return np.ascontiguousarray(got.reshape(B, HC, 2, S).transpose(0, 3, 2, 1).reshape(B, S, C))
```

```python
from contextlib import ExitStack

import numpy as np

import concourse.bass as bass
from concourse import mybir

B, S, C = 64, 128, 160
T, E = 77, 256
H, D = 20, 8
L = 4
NIP = 4
TXT = T - NIP
SCALE = float(np.float32(1.0) / np.sqrt(np.float32(D)))

HC = C // 2
HH = H // 2
NB = 4
GROUPS = B // NB
STEPS = L * NB
QH = 5
QC = QH * T

TRI = (H + 2) // 3
FIRST = T + (T + 1) // 2
CUT = FIRST - T
UC = 3 * D + 3
PPAD = 3 * T * (TRI - 1) + FIRST + 128
PCOLS = max(PPAD, H * T)
PWAVES = [(0, range(0, 4)), (1, range(0, 4)), (0, range(4, TRI)), (1, range(4, TRI))]
G2 = CUT
GC = 2 * T + (2 * T - G2)
CX = 128 + 128 + H * NIP

F32 = mybir.dt.float32
ALU = mybir.AluOpType
ACT = mybir.ActivationFunctionType
AX = mybir.AxisListType


def rows_of(kind):
    if kind == 0:
        return [(0, t) for t in range(T)] + [(1, t) for t in range(CUT)]
    return [(1, t) for t in range(CUT, T)] + [(2, t) for t in range(T)]


def heads_of(kind):
    return [tuple(h if h < H else None for h in (3 * g + kind, 3 * g + kind + 1)) for g in range(TRI)]


def build(nc, a):
    ctx = ExitStack()
    with ctx:
        def sb(name, shape):
            return ctx.enter_context(nc.sbuf_tensor(name, shape, F32))

        def pb(name, shape):
            return ctx.enter_context(nc.psum_tensor(name, shape, F32))

        def sem(name):
            return ctx.enter_context(nc.semaphore(name))

        wq = sb("wq", [128, L * 2 * C])
        wo = sb("wo", [128, L * 2 * C])
        wk = sb("wk", [128, L * 2 * C])
        wkip = sb("wkip", [128, 2 * C])
        wv = sb("wv", [128, L * 2 * 2 * TRI * 2 * D])
        wvip = sb("wvip", [128, 2 * C])
        ident = sb("ident", [128, 128])
        ones = sb("ones", [128, 128])
        fside = sb("fside", [128, 1])
        mask_k = sb("mask_k", [HC, HH])
        mask_v = sb("mask_v", [128, 2 * 2 * D])
        mask_g = sb("mask_g", [128, GC])
        mask_vip = sb("mask_vip", [H * NIP, C])

        x_in = [sb(f"x_in{b}", [128, 2 * S]) for b in range(NB)]
        x_work = [sb(f"x_work{b}", [128, 2 * S]) for b in range(NB)]
        x_out = [sb(f"x_out{b}", [HC, 2 * S]) for b in range(NB)]
        context = [sb(f"context{b}", [128, 2 * CX]) for b in range(NB)]
        k_dense = sb("k_dense", [HC, 2 * T])
        k_blocks = [sb(f"k_blocks{i}", [128, 2 * HH * T]) for i in range(2)]
        q_t = [sb(f"q_t{i}", [128, 2 * S]) for i in range(2)]
        v_rows = [sb(f"v_rows{b}", [128, 2 * TRI * UC]) for b in range(NB)]
        top = sb("top", [128, 2 * H])
        probs = [sb(f"probs{i}", [128, PCOLS]) for i in range(2)]
        probs_t = [sb(f"probs_t{i}", [128, 2 * TRI * S]) for i in range(2)]
        u_sb = sb("u_sb", [128, 2 * S])
        recip = sb("recip", [128, 3 * TRI])
        o_sb = [sb(f"o_sb{i}", [128, 3 * TRI * D]) for i in range(2)]
        o_t = sb("o_t", [128, 2 * S])
        no_ip = sb("no_ip", [128, H * NIP])
        ip_sq = sb("ip_sq", [128, 2 * NIP])
        ip_n2 = [sb(f"ip_n2{b}", [128, NIP]) for b in range(NB)]
        gram = [sb(f"gram{b}", [128, GC]) for b in range(NB)]
        v_ip = [sb(f"v_ip{b}", [H * NIP, C]) for b in range(NB)]
        s_ip = [sb(f"s_ip{b}", [128, H * NIP]) for b in range(NB)]
        weighted = sb("weighted", [128, H * T])
        q_n2 = sb("q_n2", [128, H])
        den = sb("den", [128, 3 * TRI])
        den2 = sb("den2", [128, 3 * TRI])
        rs_x = sb("rs_x", [128, H + NIP])
        rs_i = ctx.enter_context(nc.sbuf_tensor("rs_i", [128, H + NIP], mybir.dt.int32))
        rs_y = [ctx.enter_context(nc.sbuf_tensor(f"rs_y{i}", [128, H + NIP], mybir.dt.int32)) for i in range(2)]
        rs_t = sb("rs_t", [128, H + NIP])
        rs_u = sb("rs_u", [128, H + NIP])
        z_a = sb("z_a", [128, H * NIP])
        z_b = sb("z_b", [128, H * NIP])
        z_c = sb("z_c", [128, H * NIP])
        fused = sb("fused", [128, H * NIP])
        f_top = sb("f_top", [128, H])
        f_sub = sb("f_sub", [128, H * NIP])
        f_exp = sb("f_exp", [128, H * NIP])
        f_sum = sb("f_sum", [128, H])
        f_rec = sb("f_rec", [128, H])
        f_wgt = sb("f_wgt", [128, H])
        p_ip = sb("p_ip", [128, H * NIP])
        p_ip_t = sb("p_ip_t", [H * NIP, S])

        ps_s = pb("ps_s", [128, 4 * 512])
        ps_t = pb("ps_t", [128, 2 * 512])
        ps_c = pb("ps_c", [128, 512])
        ps_p = pb("ps_p", [128, 512])

        def w_half(w, l, kt, lo, n):
            at = (l * 2 + kt) * C + lo
            return w[:, at:at + n]

        def wv_half(l, kind, kt):
            n = TRI * 2 * D
            at = ((l * 2 + kind) * 2 + kt) * n
            return wv[:, at:at + n]

        def cx(b, kt, lo, n):
            return context[b][:, kt * CX + lo:kt * CX + lo + n]

        def chunk(kind, g):
            at = 3 * T * g + FIRST * kind
            return at, (kind * TRI + g) * S

        ld_w = sem("ld_w")
        ld_x = [sem(f"ld_x{b}") for b in range(NB)]
        ld_c = [sem(f"ld_c{b}") for b in range(NB)]
        st_x = [sem(f"st_x{b}") for b in range(NB)]
        setup = sem("setup")
        setup_pool = sem("setup_pool")
        k_psum = sem("k_psum")
        k_evac = sem("k_evac")
        k_ready = sem("k_ready")
        v_psum = sem("v_psum")
        v_ready = sem("v_ready")
        g_psum = sem("g_psum")
        g_ready = sem("g_ready")
        sq_ready = sem("sq_ready")
        q_psum = sem("q_psum")
        q_evac = sem("q_evac")
        s_psum = sem("s_psum")
        s_top = sem("s_top")
        s_sub = sem("s_sub")
        p_clear = sem("p_clear")
        p_ready = sem("p_ready")
        t_psum = sem("t_psum")
        t_evac = sem("t_evac")
        u_psum = sem("u_psum")
        u_evac = sem("u_evac")
        ut_psum = sem("ut_psum")
        r_ready = sem("r_ready")
        o_ready = sem("o_ready")
        ot_psum = sem("ot_psum")
        ot_evac = sem("ot_evac")
        y_psum = sem("y_psum")
        x_ready = sem("x_ready")
        w_psum = sem("w_psum")
        w_ready = sem("w_ready")
        qn_ready = sem("qn_ready")
        ip_step = sem("ip_step")
        p_marked = sem("p_marked")
        fe_ready = sem("fe_ready")
        pip_ready = sem("pip_ready")
        pipt_psum = sem("pipt_psum")
        pipt_evac = sem("pipt_evac")

        block = ctx.enter_context(nc.Block())

        primed = [x_ready, k_evac, k_ready, v_ready, g_psum, g_ready, q_evac, s_psum, s_sub, t_psum, t_evac,
                  u_psum, u_evac, ut_psum, o_ready, ot_psum, y_psum, w_psum, w_ready, fe_ready, pipt_psum,
                  pipt_evac, r_ready, s_top, k_psum, v_psum, q_psum, sq_ready, p_clear, p_marked, p_ready,
                  qn_ready, ip_step, pip_ready, ot_evac]

        def done(k, c, per=1, more=0):
            n = per * c + more + 1
            assert n > 0 or isinstance(k, int)
            return max(per * STEPS * k + n, 1) if isinstance(k, int) else k * (per * STEPS) + n

        def done_last(k, c, per=1, more=0):
            n = per * (NB * (c // STEPS) + max(0, c % STEPS - (STEPS - NB))) + more + 1
            assert n > 0 or isinstance(k, int)
            return max(per * NB * k + n, 1) if isinstance(k, int) else k * (per * NB) + n

        def layer(c):
            return c % STEPS // NB

        def last(c):
            return layer(c) == L - 1

        IP_STEPS = 21

        def run(eng, step):
            step(0, 0)
            step(0, 1)
            step(0, 2)
            with eng.Fori(0, GROUPS - 1) as k:
                for j in range(STEPS):
                    step(k, j + 3)
            for j in range(3, STEPS + 3):
                step(GROUPS - 1, j)

        def exists(k, c):
            if isinstance(k, int):
                return 0 <= STEPS * k + c < STEPS * GROUPS
            return True

        WEIGHTS = [(wq[0:HC, :], a["wq"]), (wo[0:HC, :], a["wo"]), (wk[:, :], a["wk"]),
                   (wkip[:, :], a["wkip"]), (wv[:, :], a["wv"]), (wvip[:, :], a["wvip"]),
                   (ident[:, :], a["ident"]), (fside[:, :], a["fside"]), (mask_k[:, :], a["mask_k"]),
                   (mask_v[:, :], a["mask_v"]), (mask_g[:, :], a["mask_g"]),
                   (mask_vip[:, :], a["mask_vip"])]
        N_SET, N_SET_POOL = 17, 5
        N_LD = 16 * (len(WEIGHTS) + 1 + NB)

        @block.sync
        def _(sp):
            sp.wait_ge(setup, N_SET)
            for b in range(NB):
                sp.dma_start(context[b][:, :], a["ctx"][b, :, :]).then_inc(ld_c[b], 16)
                sp.dma_start(x_in[b][0:HC, :], a["x"][b, :, :]).then_inc(ld_x[b], 16)
            with sp.Fori(0, GROUPS - 1) as k:
                for b in range(NB):
                    sp.wait_ge(x_ready, done(k, b + 1))
                    sp.dma_start(x_in[b][0:HC, :],
                                 a["x"][bass.ds(k * NB + (NB + b), 1), :, :].rearrange("a p n -> (a p) n"))\
                        .then_inc(ld_x[b], 16)
                for b in range(NB):
                    sp.wait_ge(g_psum, done_last(k, STEPS - NB + b + 1))
                    sp.dma_start(context[b][:, :],
                                 a["ctx"][bass.ds(k * NB + (NB + b), 1), :, :].rearrange("a p n -> (a p) n"))\
                        .then_inc(ld_c[b], 16)
                for b in range(NB):
                    sp.wait_ge(x_ready, done(k, STEPS - NB + b + 1))
                    sp.dma_start(a["out"][bass.ds(k * NB + b, 1), :, :].rearrange("a p n -> (a p) n"),
                                 x_out[b][:, :]).then_inc(st_x[b], 16)
            for b in range(NB):
                sp.wait_ge(x_ready, done(GROUPS - 1, STEPS - NB + b + 1))
                sp.dma_start(a["out"][(GROUPS - 1) * NB + b, :, :], x_out[b][:, :]).then_inc(st_x[b], 16)
            for b in range(NB):
                sp.wait_ge(st_x[b], 16 * GROUPS)

        @block.tensor
        def _(pe):
            def keys(k, c):
                l, b = layer(c), c % NB
                if l == 0:
                    pe.wait_ge(ld_c[b], (k + c // STEPS) * 16 + 16)
                pe.wait_ge(q_evac, done(k, c))
                n = TXT if last(c) else T
                for m in range(2):
                    for kt in range(2):
                        ins = pe.matmul(ps_p[0:HC, m * T:m * T + n], w_half(wk, l, kt, m * HC, HC),
                                        cx(b, kt, 0, n), start=kt == 0, stop=kt == 1)
                    if last(c):
                        for kt in range(2):
                            ins = pe.matmul(ps_p[0:HC, m * T + n:(m + 1) * T], w_half(wkip, 0, kt, m * HC, HC),
                                            cx(b, kt, n, NIP), start=kt == 0, stop=kt == 1)
                ins.then_inc(k_psum, 1)

            def values(k, c):
                l, b = layer(c), c % NB
                pe.wait_ge(k_evac, done(k, c + 1))
                n = TRI * 2 * D
                for kind in range(2):
                    for kt in range(2):
                        ins = pe.matmul(ps_p[:, kind * n:kind * n + n], cx(b, kt, kind * 128, 128),
                                        wv_half(l, kind, kt), start=kt == 0, stop=kt == 1)
                ins.then_inc(v_psum, 1)

            def image(k, c):
                b = c % NB
                pe.wait_ge(v_ready, done(k, c + 1))
                for kind in range(2):
                    for kt in range(2):
                        pe.matmul(ps_p[:, kind * T:(kind + 1) * T], cx(b, kt, kind * 128, 128), cx(b, kt, 0, T),
                                  start=kt == 0, stop=kt == 1)
                pe.wait_ge(sq_ready, done_last(k, c + 1))
                at = 2 * T
                for kt in range(2):
                    pe.matmul(ps_p[:, at:at + NIP], ones[:, :], ip_sq[:, kt * NIP:(kt + 1) * NIP],
                              start=kt == 0, stop=kt == 1)
                at += NIP + 2
                for kt in range(2):
                    ins = pe.matmul(ps_p[0:H * NIP, at:at + C], cx(b, kt, 256, H * NIP),
                                    wvip[:, kt * C:(kt + 1) * C], start=kt == 0, stop=kt == 1)
                ins.then_inc(g_psum, 1)

            def queries(k, c):
                l, b = layer(c), c % NB
                if last(c):
                    pe.wait_ge(g_ready, done_last(k, c + 1))
                else:
                    pe.wait_ge(v_ready, done(k, c + 1))
                if l == 0:
                    pe.wait_ge(ld_x[b], (k + c // STEPS) * 16 + 16)
                else:
                    pe.wait_ge(x_ready, done(k, c - NB + 1))
                x = x_in[b] if l == 0 else x_work[b]
                for m in range(2):
                    for kt in range(2):
                        ins = pe.matmul(ps_p[0:HC, m * S:(m + 1) * S], w_half(wq, l, kt, m * HC, HC),
                                        x[:, kt * S:(kt + 1) * S], start=kt == 0, stop=kt == 1)
                ins.then_inc(q_psum, 1)

            def scores(k, c, q):
                m = q // 2
                if q == 0:
                    pe.wait_ge(q_evac, done(k, c + 1))
                if q % 2 == 0:
                    pe.wait_ge(k_ready, done(k, c, per=2, more=m + 1))
                pe.wait_ge(s_sub, done(k, c - 1, per=4, more=q + 1))
                if last(c - 2) and exists(k, c - 2):
                    pe.wait_ge(w_ready, done_last(k, c - 2, per=4, more=q + 1))
                at = q * QC
                pe.matmul(ps_s[:, q * 512:q * 512 + QC], q_t[c % 2][:, m * S:(m + 1) * S],
                          k_blocks[c % 2][:, at:at + QC], start=True, stop=True).then_inc(s_psum, 1)

            def turn(k, c, w):
                kind, gs = PWAVES[w]
                if w == 0:
                    pe.wait_ge(p_ready, done(k, c + 1, per=4))
                    if last(c):
                        pe.wait_ge(p_clear, done_last(k, c + 1))
                pe.wait_ge(t_evac, done(k, c, per=4, more=w - 1))
                for i, g in enumerate(gs):
                    at, _ = chunk(kind, g)
                    to = (w % 2) * 512 + i * S
                    ins = pe.transpose(ps_t[:, to:to + S], probs[c % 2][:, at:at + 128], ident[:, :])
                ins.then_inc(t_psum, 1)

            def bank_free(k, c):
                if exists(k, c - 1) and last(c - 1):
                    pe.wait_ge(o_ready, done(k, c))
                else:
                    pe.wait_ge(x_ready, done(k, c))

            def product(k, c, w):
                kind, gs = PWAVES[w]
                b = c % NB
                if w == 0:
                    pe.wait_ge(v_ready, done(k, c + 1))
                    bank_free(k, c)
                pe.wait_ge(t_evac, done(k, c, per=4, more=w + 1))
                for g in gs:
                    _, at = chunk(kind, g)
                    ins = pe.matmul(ps_c[32 * (g % 4):32 * (g % 4) + UC, g // 4 * S:(g // 4 + 1) * S],
                                    v_rows[b][:, (kind * TRI + g) * UC:(kind * TRI + g + 1) * UC],
                                    probs_t[c % 2][:, at:at + S], start=kind == 0, stop=kind == 1)
                if w == 3:
                    ins.then_inc(u_psum, 1)

            def gram_product(k, c):
                b = c % NB
                pe.wait_ge(g_ready, done_last(k, c + 1))
                for z in range(4):
                    if exists(k, c + 1):
                        pe.wait_ge(s_sub, done(k, c + 1, per=4, more=z + 1))
                    else:
                        pe.wait_ge(s_sub, done(k, c, per=4, more=z + 1))
                    for g in range(2 * z, min(2 * z + 2, TRI)):
                        to = z * 512 + (g % 2) * 3 * T
                        _, at = chunk(0, g)
                        pe.matmul(ps_s[:, to:to + 2 * T], probs_t[c % 2][:, at:at + S], gram[b][:, 0:2 * T],
                                  start=g % 2 == 0, stop=False, skip_group_check=True)
                        _, at = chunk(1, g)
                        n = (2 if g == TRI - 1 else 3) * T - T - G2
                        to += T + G2
                        ins = pe.matmul(ps_s[:, to:to + n], probs_t[c % 2][:, at:at + S],
                                        gram[b][:, 2 * T:2 * T + n],
                                        start=False, stop=True, skip_group_check=True)
                    ins.then_inc(w_psum, 1)

            def turn_back(k, c):
                pe.wait_ge(u_evac, done(k, c + 1))
                if exists(k, c - 1) and last(c - 1):
                    pe.wait_ge(x_ready, done(k, c))
                for i in range(2):
                    ins = pe.transpose(ps_c[:, i * S:(i + 1) * S], u_sb[:, i * S:(i + 1) * S], ident[:, :])
                ins.then_inc(ut_psum, 1)

            def turn_image(k, c):
                pe.wait_ge(u_evac, done(k, c + 2 if exists(k, c + 1) else c + 1))
                pe.wait_ge(pip_ready, done_last(k, c + 1))
                pe.wait_ge(pipt_evac, done_last(k, c))
                pe.transpose(ps_c[0:H * NIP, 2 * S:3 * S], p_ip[:, :], ident[:, :]).then_inc(pipt_psum, 1)

            def turn_out(k, c):
                b = c % NB
                pe.wait_ge(o_ready, done(k, c + 1))
                if last(c):
                    pe.wait_ge(pipt_evac, done_last(k, c + 1))
                for m in range(2):
                    ins = pe.matmul(ps_c[0:HC, m * S:(m + 1) * S], o_sb[c % 2][:, m * HC:(m + 1) * HC], ident[:, :],
                                    is_transpose=True, start=True, stop=not last(c))
                    if last(c):
                        ins = pe.matmul(ps_c[0:HC, m * S:(m + 1) * S], v_ip[b][:, m * HC:(m + 1) * HC],
                                        p_ip_t[:, :], start=False, stop=True)
                ins.then_inc(ot_psum, 1)

            def project_out(k, c):
                l = layer(c)
                pe.wait_ge(ot_evac, done(k, c + 1))
                for m in range(2):
                    for kt in range(2):
                        ins = pe.matmul(ps_c[0:HC, m * S:(m + 1) * S], w_half(wo, l, kt, m * HC, HC),
                                        o_t[:, kt * S:(kt + 1) * S], start=kt == 0, stop=kt == 1)
                ins.then_inc(y_psum, 1)

            def step(k, c):
                now, prev, out, nxt = exists(k, c), exists(k, c - 1), exists(k, c - 2), exists(k, c + 1)
                late = exists(k, c - 3) and last(c - 3)
                soon = out and not last(c - 2)
                if late:
                    turn_image(k, c - 3)
                if now:
                    scores(k, c, 0)
                if late:
                    turn_out(k, c - 3)
                elif out:
                    turn_back(k, c - 2)
                if now:
                    scores(k, c, 1)
                if nxt:
                    keys(k, c + 1)
                if now:
                    scores(k, c, 2)
                if late:
                    project_out(k, c - 3)
                elif soon:
                    turn_out(k, c - 2)
                if now:
                    scores(k, c, 3)
                if late and out:
                    turn_back(k, c - 2)
                if nxt:
                    values(k, c + 1)
                if prev:
                    turn(k, c - 1, 0)
                    turn(k, c - 1, 1)
                if late and soon:
                    turn_out(k, c - 2)
                if nxt and last(c + 1):
                    image(k, c + 1)
                if soon:
                    project_out(k, c - 2)
                if prev:
                    turn(k, c - 1, 2)
                if nxt and not last(c + 1):
                    queries(k, c + 1)
                if prev:
                    product(k, c - 1, 0)
                    turn(k, c - 1, 3)
                    product(k, c - 1, 1)
                    product(k, c - 1, 2)
                    product(k, c - 1, 3)
                if nxt and last(c + 1):
                    queries(k, c + 1)
                if prev and last(c - 1):
                    gram_product(k, c - 1)

            pe.wait_ge(ld_w, N_LD)
            pe.wait_ge(setup, N_SET)
            pe.wait_ge(setup_pool, N_SET_POOL)
            keys(0, 0)
            values(0, 0)
            queries(0, 0)
            run(pe, step)

        @block.scalar
        def _(act):
            act.wait_ge(setup, N_SET)
            for n, (tile, src) in enumerate(WEIGHTS):
                act.dma_start(tile, src).then_inc(ld_w, 16)
            act.dma_start(wo[96:97, :], a["bias"]).then_inc(ld_w, 16)
            for b in range(NB):
                act.dma_start(v_rows[b][:, :], a["v_fixed"]).then_inc(ld_w, 16)
            act.wait_ge(ld_w, N_LD)

            def keys(k, c):
                act.wait_ge(k_psum, done(k, c + 1))
                act.wait_ge(k_ready, done(k, c, per=2))
                act.activation(k_dense[:, :], ps_p[0:HC, 0:2 * T], ACT.Copy).then_inc(k_evac, 1)

            def queries(k, c):
                act.wait_ge(q_psum, done(k, c + 1))
                act.wait_ge(s_psum, done(k, c - 1, per=4))
                act.activation(q_t[c % 2][0:HC, :], ps_p[0:HC, 0:2 * S], ACT.Copy).then_inc(q_evac, 1)

            def exps(k, c, q):
                act.wait_ge(s_sub, done(k, c, per=4, more=q + 1))
                n = TXT if last(c) else T
                p = probs[c % 2][:, q * QC:(q + 1) * QC].rearrange("p (h t) -> p h t", t=T)[:, :, 0:n]
                act.activation(p, p, ACT.Exp, scale=SCALE).then_inc(p_ready, 1)

            def turned(k, c, w):
                kind, gs = PWAVES[w]
                act.wait_ge(t_psum, done(k, c, per=4, more=w + 1))
                if w == 0:
                    act.wait_ge(u_psum, done(k, c - 1))
                    if last(c - 2) and exists(k, c - 2):
                        act.wait_ge(w_psum, done_last(k, c - 1, per=4))
                _, at = chunk(kind, gs[0])
                n = len(gs) * S
                act.activation(probs_t[c % 2][:, at:at + n], ps_t[:, (w % 2) * 512:(w % 2) * 512 + n],
                               ACT.Copy).then_inc(t_evac, 1)

            def products(k, c):
                act.wait_ge(u_psum, done(k, c + 1))
                act.wait_ge(ut_psum, done(k, c))
                act.activation(u_sb[:, :], ps_c[:, 0:2 * S], ACT.Copy).then_inc(u_evac, 1)

            def image_exp(k, c):
                act.wait_ge(ip_step, done_last(k, c, per=IP_STEPS, more=19))
                act.activation(f_exp[:, :], f_sub[:, :], ACT.Exp, scale=0.5).then_inc(fe_ready, 1)

            def image_turned(k, c):
                act.wait_ge(pipt_psum, done_last(k, c + 1))
                act.wait_ge(ot_psum, done(k, c))
                act.activation(p_ip_t[:, :], ps_c[0:H * NIP, 2 * S:3 * S], ACT.Copy).then_inc(pipt_evac, 1)

            def results(k, c):
                act.wait_ge(ot_psum, done(k, c + 1))
                act.wait_ge(y_psum, done(k, c))
                act.activation(o_t[0:HC, :], ps_c[0:HC, 0:2 * S], ACT.Copy).then_inc(ot_evac, 1)

            def step(k, c):
                now, prev, out, nxt = exists(k, c), exists(k, c - 1), exists(k, c - 2), exists(k, c + 1)
                late = exists(k, c - 3) and last(c - 3)
                soon = out and not last(c - 2)
                if out:
                    products(k, c - 2)
                if late:
                    image_turned(k, c - 3)
                    results(k, c - 3)
                if now:
                    exps(k, c, 0)
                if nxt:
                    keys(k, c + 1)
                if soon and not late:
                    results(k, c - 2)
                if now:
                    exps(k, c, 1)
                if prev:
                    turned(k, c - 1, 0)
                if now:
                    exps(k, c, 2)
                if prev:
                    turned(k, c - 1, 1)
                if soon and late:
                    results(k, c - 2)
                if prev:
                    turned(k, c - 1, 2)
                if nxt and not last(c + 1):
                    queries(k, c + 1)
                if now:
                    exps(k, c, 3)
                if prev:
                    turned(k, c - 1, 3)
                if nxt and last(c + 1):
                    queries(k, c + 1)
                if out and last(c - 2):
                    image_exp(k, c - 2)

            keys(0, 0)
            queries(0, 0)
            run(act, step)

        @block.vector
        def _(dve):
            zeros = [wq, wo, o_t, u_sb] + x_in + x_work + q_t
            sets = 0
            for tile in zeros:
                dve.memset(tile[:, :], 0.0).then_inc(setup, 1)
                sets += 1
            dve.memset(ps_c[:, :], 0.0).then_inc(setup, 1)
            dve.wait_ge(setup, sets + 1)
            dve.memset(o_t[96:97, 0:S], 1.0).then_inc(setup, 1)
            dve.memset(ones[:, :], 1.0).then_inc(setup, 1)
            assert sets + 3 == N_SET
            for i, s in enumerate(primed):
                dve.memset(z_a[:, i:i + 1], 0.0).then_inc(s, 1)
            dve.wait_ge(setup_pool, N_SET_POOL)
            dve.wait_ge(ld_w, N_LD)

            def top_of(k, c, q):
                dve.wait_ge(s_psum, done(k, c, per=4, more=q + 1))
                n = TXT if last(c) else T
                s = ps_s[:, q * 512:q * 512 + QC].rearrange("p (h t) -> p h t", t=T)
                at = (c % 2) * H + q * QH
                dve.tensor_reduce(top[:, at:at + QH], s[:, :, 0:n], AX.X, ALU.max).then_inc(s_top, 1)

            def less_top(k, c, q):
                n = TXT if last(c) else T
                s = ps_s[:, q * 512:q * 512 + QC].rearrange("p (h t) -> p h t", t=T)
                p = probs[c % 2][:, q * QC:(q + 1) * QC].rearrange("p (h t) -> p h t", t=T)
                at = (c % 2) * H + q * QH
                if q == 0:
                    dve.wait_ge(t_psum, done(k, c - 1, per=4))
                if last(c):
                    dve.tensor_copy(s_ip[c % NB][:, q * QH * NIP:(q + 1) * QH * NIP]
                                    .rearrange("p (h t) -> p h t", t=NIP), s[:, :, n:T])
                dve.wait_ge(s_top, done(k, c, per=4, more=q + 1))
                dve.tensor_tensor(p[:, :, 0:n], s[:, :, 0:n],
                                  top[:, at:at + QH].unsqueeze(2).to_broadcast([128, QH, n]),
                                  ALU.subtract).then_inc(s_sub, 1)

            def values(k, c):
                b = c % NB
                dve.wait_ge(v_psum, done(k, c + 1))
                dve.wait_ge(u_psum, done(k, c - NB + 1))
                n = TRI * 2 * D
                for kind in range(2):
                    v = v_rows[b][:, kind * TRI * UC:(kind + 1) * TRI * UC].rearrange("p (g u) -> p g u", u=UC)
                    m = mask_v[:, kind * 2 * D:(kind + 1) * 2 * D].unsqueeze(1).to_broadcast([128, TRI, 2 * D])
                    ins = dve.tensor_tensor(v[:, :, kind * D:kind * D + 2 * D],
                                            ps_p[:, kind * n:(kind + 1) * n].rearrange("p (g u) -> p g u", g=TRI),
                                            m, ALU.mult)
                ins.then_inc(v_ready, 1)

            def image_squares(k, c):
                b = c % NB
                dve.wait_ge(g_psum, done_last(k, c))
                s = context[b][:, :].rearrange("p (a n) -> p a n", a=2)[:, :, TXT:T]
                dve.tensor_tensor(ip_sq[:, :].rearrange("p (a n) -> p a n", a=2), s, s, ALU.mult)\
                   .then_inc(sq_ready, 1)

            def image_products(b):
                dve.tensor_tensor(gram[b][:, 0:2 * T].rearrange("p (h t) -> p h t", t=T),
                                  ps_p[:, 0:T].unsqueeze(1).to_broadcast([128, 2, T]),
                                  mask_g[:, 0:2 * T].rearrange("p (h t) -> p h t", t=T), ALU.mult)
                lo, mid = 2 * T, 3 * T - G2
                dve.tensor_tensor(gram[b][:, lo:mid], ps_p[:, T + G2:2 * T], mask_g[:, lo:mid], ALU.mult)
                dve.tensor_tensor(gram[b][:, mid:GC], ps_p[:, T:2 * T], mask_g[:, mid:GC], ALU.mult)\
                   .then_inc(g_ready, 1)

            def image(k, c, part):
                b = c % NB
                if part == 0:
                    dve.wait_ge(g_psum, done_last(k, c + 1))
                at = 2 * T
                if part == 1:
                    image_products(b)
                    return
                dve.tensor_scalar(ip_n2[b][:, :], ps_p[:, at:at + NIP], 1e-24, None, ALU.max)
                at += NIP + 2
                dve.tensor_tensor(v_ip[b][:, :], ps_p[0:H * NIP, at:at + C], mask_vip[:, :], ALU.mult)

            def weigh(k, c, z):
                lo, hi = 6 * z, min(6 * z + 6, H)
                if z == 0:
                    dve.wait_ge(p_marked, done_last(k, c + 1))
                dve.wait_ge(w_psum, done_last(k, c, per=4, more=z + 1))
                dve.tensor_tensor(weighted[:, lo * T:hi * T], ps_s[:, z * 512:z * 512 + (hi - lo) * T],
                                  probs[c % 2][:, lo * T:hi * T], ALU.mult).then_inc(w_ready, 1)

            def norms(k, c):
                dve.wait_ge(w_ready, done_last(k, c + 1, per=4))
                dve.tensor_reduce(q_n2[:, :], weighted[:, :].rearrange("p (h t) -> p h t", t=T)[:, :, 0:TXT],
                                  AX.X, ALU.add).then_inc(qn_ready, 1)

            def results(k, c):
                u = ps_c[:, 0:TRI * 32].rearrange("p (g x) -> p g x", x=32)
                dve.wait_ge(ut_psum, done(k, c + 1))
                dve.reciprocal(recip[:, :].rearrange("p (g i) -> p g i", i=3), u[:, :, 3 * D:3 * D + 3])\
                   .then_inc(r_ready, 1)
                if last(c):
                    image_branch(k, c, 0)
                dve.wait_ge(r_ready, done(k, c + 1))
                dve.wait_ge(ot_psum, done(k, c - 1))
                ins = dve.tensor_tensor(o_sb[c % 2][:, :].rearrange("p (g i d) -> p g i d", i=3, d=D),
                                        u[:, :, 0:3 * D].rearrange("p g (i d) -> p g i d", d=D),
                                        recip[:, :].rearrange("p (g i) -> p g i", i=3).unsqueeze(3)
                                        .to_broadcast([128, TRI, 3, D]), ALU.mult)
                ins.then_inc(o_ready, 1)

            def image_branch(k, c, n):
                b = c % NB

                def per_head(ap):
                    return ap.unsqueeze(2).to_broadcast([128, H, NIP])

                def per_token(ap):
                    return ap[:, :].rearrange("p (h t) -> p h t", t=NIP)

                if n > 0:
                    dve.wait_ge(ip_step, done_last(k, c, per=IP_STEPS, more=n))
                y, y_new = rs_y[n // 3 % 2], rs_y[(n // 3 + 1) % 2]
                if n == 0:
                    u = ps_c[:, 0:TRI * 32].rearrange("p (g x) -> p g x", x=32)
                    dve.tensor_copy(den[:, :].rearrange("p (g i) -> p g i", i=3), u[:, :, 3 * D:3 * D + 3])\
                       .then_inc(ip_step, 1)
                    return
                if n == 1:
                    dve.wait_ge(w_ready, done_last(k, c + 1, per=4))
                    dve.tensor_copy(per_token(z_a),
                                    weighted[:, :].rearrange("p (h t) -> p h t", t=T)[:, :, TXT:T])
                    ins = dve.scalar_tensor_tensor(out=den2[:, :], in0=den[:, :], scalar=1e-24, in1=den[:, :],
                                                   op0=ALU.mult, op1=ALU.mult)
                elif n == 2:
                    dve.wait_ge(qn_ready, done_last(k, c + 1))
                    dve.tensor_copy(rs_x[:, H:H + NIP], ip_n2[b][:, :])
                    ins = dve.tensor_tensor(rs_x[:, 0:H], q_n2[:, :], den2[:, 0:H], ALU.max)
                elif n == 3:
                    ins = dve.tensor_scalar(rs_i[:, :], rs_x[:, :].bitcast(mybir.dt.int32), 1, None,
                                            ALU.logical_shift_right)
                elif n == 4:
                    ins = dve.tensor_scalar(rs_y[1][:, :], rs_i[:, :], -1.0, float(0x5F3759DF), ALU.mult, ALU.add)
                elif n < 14 and n % 3 == 2:
                    ins = dve.scalar_tensor_tensor(out=rs_t[:, :], in0=rs_x[:, :], scalar=-0.5,
                                                   in1=y[:, :].bitcast(F32), op0=ALU.mult, op1=ALU.mult)
                elif n < 14 and n % 3 == 0:
                    y = rs_y[(n // 3 - 1) % 2]
                    ins = dve.tensor_tensor(rs_u[:, :], rs_t[:, :], y[:, :].bitcast(F32), ALU.mult)
                elif n < 14:
                    y, y_new = rs_y[(n // 3 - 1) % 2], rs_y[n // 3 % 2]
                    ins = dve.scalar_tensor_tensor(out=y_new[:, :].bitcast(F32), in0=rs_u[:, :], scalar=1.5,
                                                   in1=y[:, :].bitcast(F32), op0=ALU.add, op1=ALU.mult)
                elif n == 14:
                    y = rs_y[0]
                    ins = dve.tensor_tensor(per_token(z_b), per_token(z_a), per_head(y[:, 0:H].bitcast(F32)), ALU.mult)
                elif n == 15:
                    y = rs_y[0]
                    ins = dve.tensor_tensor(per_token(z_c), per_token(z_b), y[:, H:H + NIP].bitcast(F32).unsqueeze(1)
                                            .to_broadcast([128, H, NIP]), ALU.mult)
                elif n == 16:
                    ins = dve.scalar_tensor_tensor(out=fused[:, :], in0=s_ip[b][:, :], scalar=2.0 * SCALE,
                                                   in1=z_c[:, :], op0=ALU.mult, op1=ALU.add)
                elif n == 17:
                    ins = dve.tensor_reduce(f_top[:, :], per_token(fused), AX.X, ALU.max)
                elif n == 18:
                    dve.wait_ge(fe_ready, done_last(k, c))
                    ins = dve.tensor_tensor(per_token(f_sub), per_token(fused), per_head(f_top[:, :]), ALU.subtract)
                elif n == 19:
                    dve.wait_ge(fe_ready, done_last(k, c + 1))
                    ins = dve.tensor_reduce(f_sum[:, :], per_token(f_exp), AX.X, ALU.add)
                elif n == 20:
                    ins = dve.reciprocal(f_rec[:, :], f_sum[:, :])
                ins.then_inc(ip_step, 1)

            def image_weights(k, c):
                dve.wait_ge(ip_step, done_last(k, c + 1, per=IP_STEPS))
                dve.wait_ge(pipt_psum, done_last(k, c))
                f = f_rec[:, :].unsqueeze(2).to_broadcast([128, H, NIP])
                dve.scalar_tensor_tensor(out=p_ip[:, :].rearrange("p (h t) -> p h t", t=NIP),
                                         in0=f_exp[:, :].rearrange("p (h t) -> p h t", t=NIP),
                                         scalar=fside[:, 0:1], in1=f, op0=ALU.mult, op1=ALU.mult)\
                   .then_inc(pip_ready, 1)

            def new_x(k, c):
                l, b = layer(c), c % NB
                dve.wait_ge(y_psum, done(k, c + 1))
                old = x_in[b] if l == 0 else x_work[b]
                to = x_out[b] if l == L - 1 else x_work[b]
                if l == L - 1:
                    n = c // STEPS * 16
                    if isinstance(k, int):
                        n += k * 16
                        if n > 0:
                            dve.wait_ge(st_x[b], n)
                    else:
                        dve.wait_ge(st_x[b], k * 16 + n)
                dve.tensor_tensor(to[0:HC, :], ps_c[0:HC, 0:2 * S], old[0:HC, :], ALU.add).then_inc(x_ready, 1)

            def step(k, c):
                now, prev, out, nxt = exists(k, c), exists(k, c - 1), exists(k, c - 2), exists(k, c + 1)
                late = exists(k, c - 3) and last(c - 3)

                def image_steps(lo, hi):
                    if out and last(c - 2):
                        for n in range(lo, hi):
                            image_branch(k, c - 2, n)

                def scored(q):
                    if now:
                        top_of(k, c, q)
                        less_top(k, c, q)

                if now:
                    top_of(k, c, 0)
                if out and not late:
                    results(k, c - 2)
                if now:
                    less_top(k, c, 0)
                if out and last(c - 2):
                    norms(k, c - 2)
                if nxt and last(c + 1):
                    image_squares(k, c + 1)
                scored(1)
                if late:
                    new_x(k, c - 3)
                scored(2)
                if late and out:
                    results(k, c - 2)
                image_steps(1, 3)
                if nxt:
                    values(k, c + 1)
                image_steps(3, 4)
                if now:
                    top_of(k, c, 3)
                image_steps(4, 5)
                if now:
                    less_top(k, c, 3)
                image_steps(5, 6)
                if nxt and last(c + 1):
                    image(k, c + 1, 0)
                    image_steps(6, 7)
                    image(k, c + 1, 1)
                    image_steps(7, 8)
                else:
                    image_steps(6, 8)
                if out and not last(c - 2):
                    new_x(k, c - 2)
                image_steps(8, 19)
                if prev and last(c - 1):
                    weigh(k, c - 1, 0)
                image_steps(19, 21)
                if out and last(c - 2):
                    image_weights(k, c - 2)
                if prev and last(c - 1):
                    for z in range(1, 4):
                        weigh(k, c - 1, z)

            values(0, 0)
            run(dve, step)

        @block.gpsimd
        def _(pool):
            for n in range(2):
                pool.memset(k_blocks[n][:, :], 0.0).then_inc(setup_pool, 1)
                pool.memset(probs[n][:, :], 0.0).then_inc(setup_pool, 1)
            pool.memset(no_ip[:, :], 0.0).then_inc(setup_pool, 1)
            pool.wait_ge(setup, N_SET)
            pool.wait_ge(setup_pool, N_SET_POOL)
            pool.wait_ge(ld_w, N_LD)

            def clear(k, c):
                pool.wait_ge(t_psum, done(k, c - 1, per=4))
                if last(c - 2) and exists(k, c - 2):
                    pool.wait_ge(w_ready, done_last(k, c - 1, per=4))
                z = no_ip[:, :].rearrange("p (h t) -> p h t", t=NIP)
                pool.tensor_tensor(probs[c % 2][:, 0:H * T].rearrange("p (h t) -> p h t", t=T)[:, :, TXT:T],
                                   z, z, ALU.mult).then_inc(p_clear, 1)

            def mark(k, c):
                pool.wait_ge(t_psum, done(k, c + 1, per=4))
                one = ones[:, 0:H * NIP].rearrange("p (h t) -> p h t", t=NIP)
                pool.tensor_tensor(probs[c % 2][:, 0:H * T].rearrange("p (h t) -> p h t", t=T)[:, :, TXT:T],
                                   one, one, ALU.mult).then_inc(p_marked, 1)

            def keys(k, c):
                pool.wait_ge(k_evac, done(k, c + 1))
                pool.wait_ge(s_psum, done(k, c - 1, per=4))
                for m in range(2):
                    pool.tensor_tensor(k_blocks[c % 2][0:HC, m * HH * T:(m + 1) * HH * T]
                                       .rearrange("p (h t) -> p h t", t=T),
                                       k_dense[:, m * T:(m + 1) * T].unsqueeze(1).to_broadcast([HC, HH, T]),
                                       mask_k[:, :].unsqueeze(2).to_broadcast([HC, HH, T]),
                                       ALU.mult).then_inc(k_ready, 1)

            def step(k, c):
                if exists(k, c) and last(c):
                    clear(k, c)
                if exists(k, c + 1):
                    keys(k, c + 1)
                if exists(k, c - 1) and last(c - 1):
                    mark(k, c - 1)

            keys(0, 0)
            run(pool, step)



def _halves(w, rows):
    return w.reshape(2, rows, w.shape[-1]).transpose(1, 0, 2)


def _layout(inputs):
    f = {k: np.asarray(v) for k, v in inputs.items()}
    n = {"q": ["L0_xattn_to_q_w", "L1_xattn_Wq", "L2_xattn_Wq", "L3_xattn_W_q"],
         "k": ["L0_xattn_to_k_w", "L1_xattn_Wk", "L2_xattn_Wk", "L3_xattn_W_k"],
         "v": ["L0_xattn_to_v_w", "L1_xattn_Wv", "L2_xattn_Wv", "L3_xattn_W_v"],
         "o": ["L0_xattn_to_out_w", "L1_xattn_Wout", "L2_xattn_Wo", "L3_xattn_W_out"],
         "b": ["L0_xattn_to_out_b", "L1_xattn_bout", "L2_xattn_bo", "L3_xattn_b_out"]}

    def weights(kind):
        return [f[name].T if l == 2 else f[name] for l, name in enumerate(n[kind])]

    out = {}
    x = f["x"]
    dt = x.dtype
    out["x"] = x.reshape(B, S, 2, HC).transpose(0, 3, 2, 1).reshape(B, HC, 2 * S)
    ct = f["ctx_2048"].reshape(B, T, 2, 128).transpose(0, 3, 2, 1)
    cx = np.zeros((B, 128, 2, CX), dt)
    for kind in range(2):
        toks = [t for _, t in rows_of(kind)]
        cx[:, :, :, kind * 128:kind * 128 + len(toks)] = ct[:, :, :, toks]
    cx[:, :, :, 256:] = ct[:, :, :, [TXT + i % NIP for i in range(H * NIP)]]
    out["ctx"] = cx.reshape(B, 128, 2 * CX)
    out["wq"] = np.stack([_halves(w, HC) for w in weights("q")], 1).reshape(HC, -1)
    out["wo"] = np.stack([_halves(w, HC) for w in weights("o")], 1).reshape(HC, -1)
    out["wk"] = np.stack([_halves(w, 128) for w in weights("k")], 1).reshape(128, -1)
    out["wkip"] = _halves(f["L3_xattn_W_k_ip"], 128).reshape(128, -1)
    out["wvip"] = _halves(f["L3_xattn_W_v_ip"], 128).reshape(128, -1)
    wv = np.zeros((128, L, 2, 2, TRI, 2, D), dt)
    for l, w in enumerate(weights("v")):
        w = _halves(w, 128).reshape(128, 2, H, D)
        for kind in range(2):
            for g, pair in enumerate(heads_of(kind)):
                for i, h in enumerate(pair):
                    if h is not None:
                        wv[:, l, kind, :, g, i] = w[:, :, h]
    out["wv"] = wv.reshape(128, -1)
    bias = np.zeros((1, L, 2, C), dt)
    for l, name in enumerate(n["b"]):
        bias[0, l, 0] = f[name]
    out["bias"] = bias.reshape(1, -1)
    out["fside"] = f["fside_S_0"].reshape(S, 1)
    out["ident"] = np.eye(128, dtype=dt)
    out["mask_k"] = np.kron(np.eye(HH, dtype=dt), np.ones((D, 1), dt))
    out["mask_vip"] = np.kron(np.eye(H, dtype=dt), np.ones((NIP, D), dt))
    mv = np.zeros((128, 2, 2, D), dt)
    mg = [np.zeros((128, 2, T), dt) for _ in range(2)]
    vf = np.zeros((128, 2, TRI, UC), dt)
    for kind in range(2):
        for r, (h, t) in enumerate(rows_of(kind)):
            mv[r, kind, h - kind] = 1
            if t < TXT:
                mg[kind][r, h - kind] = 1
                if kind == 0 and h == 1:
                    mg[kind][r, 1, CUT:TXT] = 2
            vf[r, kind, :, 3 * D + h] = 1
            if h == 1:
                vf[r, kind, TRI - 1, 3 * D + 2] = 1
    out["mask_v"] = mv.reshape(128, -1)
    out["mask_g"] = np.concatenate([mg[0].reshape(128, -1), mg[1].reshape(128, -1)[:, G2:]], 1)
    out["v_fixed"] = vf.reshape(128, -1)
    return {k: np.ascontiguousarray(v) for k, v in out.items()}


def kernel(**inputs):
    import concourse.bacc as bacc
    from concourse.bass_utils import run_bass_kernel_spmd

    nc = bacc.Bacc("TRN2", target_bir_lowering=False, num_devices=1)
    arrays, tensors = {}, {}
    for name, v in _layout(inputs).items():
        arrays[f"in_{name}"] = v
        tensors[name] = nc.dram_tensor(f"in_{name}", v.shape, mybir.dt.from_np(v.dtype), kind="ExternalInput").ap()
    tensors["out"] = nc.dram_tensor("out_x", (B, HC, 2 * S), F32, kind="ExternalOutput").ap()
    build(nc, tensors)
    r = run_bass_kernel_spmd(nc, [arrays], core_ids=[0])
    got = np.asarray(r.results[0]["out_x"])
    return np.ascontiguousarray(got.reshape(B, HC, 2, S).transpose(0, 3, 2, 1).reshape(B, S, C))
```

```python
from contextlib import ExitStack

import numpy as np

import concourse.bass as bass
from concourse import mybir

B, S, C = 64, 128, 160
T, E = 77, 256
H, D = 20, 8
L = 4
NIP = 4
TXT = T - NIP
SCALE = float(np.float32(1.0) / np.sqrt(np.float32(D)))

HC = C // 2
HH = H // 2
NB = 4
GROUPS = B // NB
STEPS = L * NB
QH = 5
QC = QH * T
QE = QC + QC % 2
CQ = C // 4
PARTS = 3
THIRD = 64 - CQ
KROWS = 64 + CQ
QROWS = PARTS * CQ

TRI = (H + 2) // 3
FIRST = T + (T + 1) // 2
CUT = FIRST - T
UC = 3 * D + 3
PPAD = 3 * T * (TRI - 1) + FIRST + 128
PCOLS = max(PPAD, H * T)
PWAVES = [(0, range(0, 4)), (1, range(0, 4)), (0, range(4, TRI)), (1, range(4, TRI))]
G2 = CUT
FOLD = TXT // 2
GC = 2 * T + (2 * T - G2)
CX = 128 + 128 + H * NIP

F32 = mybir.dt.float32
F32R = mybir.dt.float32r
ALU = mybir.AluOpType
ACT = mybir.ActivationFunctionType
AX = mybir.AxisListType


def rows_of(kind):
    if kind == 0:
        return [(0, t) for t in range(T)] + [(1, t) for t in range(CUT)]
    return [(1, t) for t in range(CUT, T)] + [(2, t) for t in range(T)]


def heads_of(kind):
    return [tuple(h if h < H else None for h in (3 * g + kind, 3 * g + kind + 1)) for g in range(TRI)]


def build(nc, a):
    ctx = ExitStack()
    with ctx:
        def sb(name, shape, dtype=F32):
            return ctx.enter_context(nc.sbuf_tensor(name, shape, dtype))

        def pb(name, shape):
            return ctx.enter_context(nc.psum_tensor(name, shape, F32))

        def sem(name):
            return ctx.enter_context(nc.semaphore(name))

        wq = sb("wq", [128, L * 4 * QROWS])
        wo = sb("wo", [128, L * 2 * C])
        wk = sb("wk", [128, L * 4 * KROWS])
        wkip = sb("wkip", [128, 4 * KROWS])
        wv = sb("wv", [128, L * 2 * 2 * TRI * 2 * D])
        wvip = sb("wvip", [128, 2 * C])
        ident = sb("ident", [128, 128])
        ones = sb("ones", [128, 128])
        fside = sb("fside", [128, 1])
        mask_k = sb("mask_k", [QROWS, QH])
        mask_v = sb("mask_v", [128, 2 * 2 * D])
        mask_g = sb("mask_g", [128, GC])
        mask_vip = sb("mask_vip", [H * NIP, C])

        x_in = [sb(f"x_in{b}", [128, 2 * S]) for b in range(NB)]
        x_work = [sb(f"x_work{b}", [128, 2 * S]) for b in range(NB)]
        x_out = [sb(f"x_out{b}", [HC, 2 * S]) for b in range(NB)]
        context = [sb(f"context{b}", [128, 2 * CX]) for b in range(NB)]
        k_low = sb("k_low", [KROWS, 2 * T], F32R)
        k_stack = [sb(f"k_stack{i}", [QROWS, 2 * 2 * T], F32R) for i in range(2)]
        q_stack = [sb(f"q_stack{i}", [QROWS, 2 * 2 * S], F32R) for i in range(2)]
        k_blocks = [sb(f"k_blocks{i}", [QROWS, 4 * QE], F32R) for i in range(2)]
        v_rows = [sb(f"v_rows{b}", [128, 2 * TRI * UC]) for b in range(NB)]
        top = sb("top", [128, 2 * H])
        probs = [sb(f"probs{i}", [128, PCOLS]) for i in range(2)]
        probs_t = [sb(f"probs_t{i}", [128, 2 * TRI * S]) for i in range(2)]
        u_sb = sb("u_sb", [128, 2 * S])
        recip = sb("recip", [128, 3 * TRI])
        o_sb = [sb(f"o_sb{i}", [128, 3 * TRI * D]) for i in range(2)]
        o_t = sb("o_t", [128, 2 * S])
        no_ip = sb("no_ip", [128, H * NIP])
        ip_sq = sb("ip_sq", [128, 2 * NIP])
        ip_n2 = [sb(f"ip_n2{b}", [128, NIP]) for b in range(NB)]
        gram = [sb(f"gram{b}", [128, GC]) for b in range(NB)]
        v_ip = [sb(f"v_ip{b}", [H * NIP, C]) for b in range(NB)]
        s_ip = [sb(f"s_ip{b}", [128, H * NIP]) for b in range(NB)]
        weighted = sb("weighted", [128, H * T])
        q_n2 = sb("q_n2", [128, H])
        den = sb("den", [128, 3 * TRI])
        den2 = sb("den2", [128, 3 * TRI])
        rs_x = sb("rs_x", [128, H + NIP])
        rs_i = ctx.enter_context(nc.sbuf_tensor("rs_i", [128, H + NIP], mybir.dt.int32))
        rs_y = [ctx.enter_context(nc.sbuf_tensor(f"rs_y{i}", [128, H + NIP], mybir.dt.int32)) for i in range(2)]
        rs_t = sb("rs_t", [128, H + NIP])
        rs_u = sb("rs_u", [128, H + NIP])
        z_a = sb("z_a", [128, H * NIP])
        z_b = sb("z_b", [128, H * NIP])
        z_c = sb("z_c", [128, H * NIP])
        fused = sb("fused", [128, H * NIP])
        f_top = sb("f_top", [128, H])
        f_sub = sb("f_sub", [128, H * NIP])
        f_exp = sb("f_exp", [128, H * NIP])
        f_sum = sb("f_sum", [128, H])
        f_rec = sb("f_rec", [128, H])
        f_wgt = sb("f_wgt", [128, H])
        p_ip = sb("p_ip", [128, H * NIP])
        p_ip_t = sb("p_ip_t", [H * NIP, S])

        ps_s = pb("ps_s", [128, 4 * 512])
        ps_t = pb("ps_t", [128, 2 * 512])
        ps_c = pb("ps_c", [128, 512])
        ps_p = pb("ps_p", [128, 512])

        def w_half(w, l, kt, lo, n):
            at = (l * 2 + kt) * C + lo
            return w[:, at:at + n]

        def w_rows(w, l, kt, m, n):
            at = ((l * 2 + kt) * 2 + m) * n
            return w[:, at:at + n]

        def wv_half(l, kind, kt):
            n = TRI * 2 * D
            at = ((l * 2 + kind) * 2 + kt) * n
            return wv[:, at:at + n]

        def cx(b, kt, lo, n):
            return context[b][:, kt * CX + lo:kt * CX + lo + n]

        def chunk(kind, g):
            at = 3 * T * g + FIRST * kind
            return at, (kind * TRI + g) * S

        ld_w = sem("ld_w")
        ld_x = [sem(f"ld_x{b}") for b in range(NB)]
        ld_c = [sem(f"ld_c{b}") for b in range(NB)]
        st_x = [sem(f"st_x{b}") for b in range(NB)]
        setup = sem("setup")
        setup_pool = sem("setup_pool")
        k_psum = sem("k_psum")
        k_evac = sem("k_evac")
        k_split = sem("k_split")
        k_moved = sem("k_moved")
        k_ready = sem("k_ready")
        v_psum = sem("v_psum")
        v_ready = sem("v_ready")
        g_psum = sem("g_psum")
        g_ready = sem("g_ready")
        sq_ready = sem("sq_ready")
        q_psum = sem("q_psum")
        q_evac = sem("q_evac")
        q_split = sem("q_split")
        q_moved = sem("q_moved")
        s_psum = sem("s_psum")
        s_top = sem("s_top")
        s_sub = sem("s_sub")
        p_clear = sem("p_clear")
        p_ready = sem("p_ready")
        t_psum = sem("t_psum")
        t_evac = sem("t_evac")
        u_psum = sem("u_psum")
        u_evac = sem("u_evac")
        ut_psum = sem("ut_psum")
        r_ready = sem("r_ready")
        o_ready = sem("o_ready")
        ot_psum = sem("ot_psum")
        ot_evac = sem("ot_evac")
        y_psum = sem("y_psum")
        x_ready = sem("x_ready")
        w_psum = sem("w_psum")
        w_ready = sem("w_ready")
        w_folded = sem("w_folded")
        qn_ready = sem("qn_ready")
        ip_step = sem("ip_step")
        p_marked = sem("p_marked")
        fe_ready = sem("fe_ready")
        pip_ready = sem("pip_ready")
        pipt_psum = sem("pipt_psum")
        pipt_evac = sem("pipt_evac")

        block = ctx.enter_context(nc.Block())

        primed = [x_ready, k_evac, k_split, q_split, w_folded, k_moved, q_moved, k_ready, v_ready, g_psum, g_ready,
                  q_evac, s_psum, s_sub, t_psum, t_evac, u_psum, u_evac, ut_psum, o_ready,
                  ot_psum, y_psum, w_psum, w_ready, fe_ready, pipt_psum, pipt_evac, r_ready,
                  s_top, k_psum, v_psum, q_psum, sq_ready, p_clear, p_marked, p_ready, qn_ready,
                  ip_step, pip_ready, ot_evac]

        def done(k, c, per=1, more=0):
            n = per * c + more + 1
            assert n > 0 or isinstance(k, int)
            return max(per * STEPS * k + n, 1) if isinstance(k, int) else k * (per * STEPS) + n

        def done_last(k, c, per=1, more=0):
            n = per * (NB * (c // STEPS) + max(0, c % STEPS - (STEPS - NB))) + more + 1
            assert n > 0 or isinstance(k, int)
            return max(per * NB * k + n, 1) if isinstance(k, int) else k * (per * NB) + n

        def layer(c):
            return c % STEPS // NB

        def last(c):
            return layer(c) == L - 1

        IP_STEPS = 21

        def run(eng, step):
            step(0, 0)
            step(0, 1)
            step(0, 2)
            with eng.Fori(0, GROUPS - 1) as k:
                for j in range(STEPS):
                    step(k, j + 3)
            for j in range(3, STEPS + 3):
                step(GROUPS - 1, j)

        def exists(k, c):
            if isinstance(k, int):
                return 0 <= STEPS * k + c < STEPS * GROUPS
            return True

        def plain(c):
            return 3 <= c % STEPS < STEPS - NB - 1

        def final(k, c):
            return exists(k, c - 3) and last(c - 3) and not last(c - 2)

        def deferred(c):
            return plain(c + 1) and plain(c + 2)

        WEIGHTS = [(wq[0:HC, :], a["wq"]), (wo[0:HC, :], a["wo"]), (wk[:, :], a["wk"]),
                   (wkip[:, :], a["wkip"]), (wv[:, :], a["wv"]), (wvip[:, :], a["wvip"]),
                   (ident[:, :], a["ident"]), (fside[:, :], a["fside"]), (mask_k[:, :], a["mask_k"]),
                   (mask_v[:, :], a["mask_v"]), (mask_g[:, :], a["mask_g"]),
                   (mask_vip[:, :], a["mask_vip"])]
        N_SET, N_SET_POOL = 15, 5
        N_LD = 16 * (len(WEIGHTS) + 1 + NB)

        @block.sync
        def _(sp):
            sp.wait_ge(setup, N_SET)
            for b in range(NB):
                sp.dma_start(context[b][:, :], a["ctx"][b, :, :]).then_inc(ld_c[b], 16)
                sp.dma_start(x_in[b][0:HC, :], a["x"][b, :, :]).then_inc(ld_x[b], 16)

            def third(to, source, q, m, moved):
                lo = 64 * q
                sp.dma_start(to[CQ:64, q * m:(q + 1) * m].bitcast(F32),
                             source[lo:lo + THIRD, :].bitcast(F32)).then_inc(moved, 16)
                sp.dma_start(to[KROWS:QROWS, q * m:(q + 1) * m].bitcast(F32),
                             source[lo + THIRD:lo + CQ, :].bitcast(F32)).then_inc(moved, 16)

            def queries(k, c):
                sp.wait_ge(q_split, done(k, c + 1))
                q = q_stack[c % 2]
                third(q, q[:, 2 * S:4 * S], 1, 2 * S, q_moved)

            def keys(k, c):
                sp.wait_ge(k_split, done(k, c + 1))
                for q in range(2):
                    third(k_stack[c % 2], k_low, q, 2 * T, k_moved)

            def next_x(k, b):
                sp.wait_ge(x_ready, done(k, b + 1))
                sp.dma_start(x_in[b][0:HC, :],
                             a["x"][bass.ds(k * NB + (NB + b), 1), :, :].rearrange("a p n -> (a p) n"))\
                    .then_inc(ld_x[b], 16)

            def next_context(k, b):
                sp.wait_ge(g_psum, done_last(k, STEPS - NB + b + 1))
                sp.dma_start(context[b][:, :],
                             a["ctx"][bass.ds(k * NB + (NB + b), 1), :, :].rearrange("a p n -> (a p) n"))\
                    .then_inc(ld_c[b], 16)

            def store(k, b):
                sp.wait_ge(x_ready, done(k, STEPS - NB + b + 1))
                if isinstance(k, int):
                    out = a["out"][k * NB + b, :, :]
                else:
                    out = a["out"][bass.ds(k * NB + b, 1), :, :].rearrange("a p n -> (a p) n")
                sp.dma_start(out, x_out[b][:, :]).then_inc(st_x[b], 16)

            def step(k, c):
                if exists(k, c + 1):
                    queries(k, c + 1)
                if exists(k, c + 2):
                    keys(k, c + 2)
                if not isinstance(k, int):
                    if NB <= c < 2 * NB:
                        next_x(k, c - NB)
                    if STEPS - NB <= c < STEPS:
                        next_context(k, c - (STEPS - NB))
                if c >= STEPS - 1:
                    store(k, c - (STEPS - 1))

            keys(0, 0)
            queries(0, 0)
            keys(0, 1)
            run(sp, step)
            for b in range(NB):
                sp.wait_ge(st_x[b], 16 * GROUPS)

        @block.tensor
        def _(pe):
            def keys(k, c):
                l, b = layer(c), c % NB
                if l == 0:
                    pe.wait_ge(ld_c[b], (k + c // STEPS) * 16 + 16)
                if exists(k, c - 1) and last(c - 1):
                    pe.wait_ge(g_ready, done_last(k, c))
                else:
                    pe.wait_ge(v_ready, done(k, c))
                n = TXT if last(c) else T
                for m in range(2):
                    for kt in range(2):
                        ins = pe.matmul(ps_p[0:KROWS, m * T:m * T + n], w_rows(wk, l, kt, m, KROWS),
                                        cx(b, kt, 0, n), start=kt == 0, stop=kt == 1)
                    if last(c):
                        for kt in range(2):
                            ins = pe.matmul(ps_p[0:KROWS, m * T + n:(m + 1) * T], w_rows(wkip, 0, kt, m, KROWS),
                                            cx(b, kt, n, NIP), start=kt == 0, stop=kt == 1)
                ins.then_inc(k_psum, 1)

            def values(k, c):
                l, b = layer(c), c % NB
                pe.wait_ge(q_split, done(k, c + 1))
                n = TRI * 2 * D
                for kind in range(2):
                    for kt in range(2):
                        ins = pe.matmul(ps_p[:, kind * n:kind * n + n], cx(b, kt, kind * 128, 128),
                                        wv_half(l, kind, kt), start=kt == 0, stop=kt == 1)
                ins.then_inc(v_psum, 1)

            def image(k, c):
                b = c % NB
                pe.wait_ge(v_ready, done(k, c + 1))
                for kind in range(2):
                    for kt in range(2):
                        pe.matmul(ps_p[:, kind * T:(kind + 1) * T], cx(b, kt, kind * 128, 128), cx(b, kt, 0, T),
                                  start=kt == 0, stop=kt == 1)
                pe.wait_ge(sq_ready, done_last(k, c + 1))
                at = 2 * T
                for kt in range(2):
                    pe.matmul(ps_p[:, at:at + NIP], ones[:, :], ip_sq[:, kt * NIP:(kt + 1) * NIP],
                              start=kt == 0, stop=kt == 1)
                at += NIP + 2
                for kt in range(2):
                    ins = pe.matmul(ps_p[0:H * NIP, at:at + C], cx(b, kt, 256, H * NIP),
                                    wvip[:, kt * C:(kt + 1) * C], start=kt == 0, stop=kt == 1)
                ins.then_inc(g_psum, 1)

            def queries(k, c):
                l, b = layer(c), c % NB
                if exists(k, c - 1) and not exists(k, c + 1) and last(c - 1):
                    pe.wait_ge(g_ready, done_last(k, c))
                pe.wait_ge(k_split, done(k, c + 1))
                if l == 0:
                    pe.wait_ge(ld_x[b], (k + c // STEPS) * 16 + 16)
                else:
                    pe.wait_ge(x_ready, done(k, c - NB + 1))
                x = x_in[b] if l == 0 else x_work[b]
                for m in range(2):
                    for kt in range(2):
                        ins = pe.matmul(ps_p[0:QROWS, m * S:(m + 1) * S], w_rows(wq, l, kt, m, QROWS),
                                        x[:, kt * S:(kt + 1) * S], start=kt == 0, stop=kt == 1)
                ins.then_inc(q_psum, 1)

            def scores(k, c, q):
                m, j = q // 2, q % 2
                if q == 0:
                    pe.wait_ge(q_moved, done(k, c + 1, per=16 * 2))
                pe.wait_ge(k_ready, done(k, c, per=4, more=q + 1))
                pe.wait_ge(s_sub, done(k, c - 1, per=4, more=q + 1))
                if last(c - 2) and exists(k, c - 2):
                    pe.wait_ge(w_ready, done_last(k, c - 2, per=4, more=q + 1))
                at = (j * 2 + m) * S
                pe.matmul(ps_s[:, q * 512:q * 512 + QE], q_stack[c % 2][:, at:at + S],
                          k_blocks[c % 2][:, q * QE:(q + 1) * QE], start=True, stop=True).then_inc(s_psum, 1)

            def early(k, c):
                return exists(k, c - 1) and not (exists(k, c - 2) and last(c - 2))

            def turn(k, c, w):
                kind, gs = PWAVES[w]
                if w == 0:
                    pe.wait_ge(p_ready, done(k, c + 1, per=4))
                    if last(c):
                        pe.wait_ge(p_clear, done_last(k, c + 1))
                pe.wait_ge(t_evac, done(k, c, per=4, more=w - 1))
                for i, g in enumerate(gs):
                    at, _ = chunk(kind, g)
                    to = (w % 2) * 512 + i * S
                    ins = pe.transpose(ps_t[:, to:to + S], probs[c % 2][:, at:at + 128], ident[:, :])
                ins.then_inc(t_psum, 1)

            def bank_free(k, c):
                if exists(k, c - 1) and last(c - 1):
                    pe.wait_ge(o_ready, done(k, c))
                else:
                    pe.wait_ge(x_ready, done(k, c))

            def product(k, c, w):
                kind, gs = PWAVES[w]
                b = c % NB
                if w == 0:
                    pe.wait_ge(v_ready, done(k, c + 1))
                    bank_free(k, c)
                pe.wait_ge(t_evac, done(k, c, per=4, more=w + 1))
                for g in gs:
                    _, at = chunk(kind, g)
                    ins = pe.matmul(ps_c[32 * (g % 4):32 * (g % 4) + UC, g // 4 * S:(g // 4 + 1) * S],
                                    v_rows[b][:, (kind * TRI + g) * UC:(kind * TRI + g + 1) * UC],
                                    probs_t[c % 2][:, at:at + S], start=kind == 0, stop=kind == 1)
                if w == 3:
                    ins.then_inc(u_psum, 1)

            def gram_product(k, c):
                b = c % NB
                pe.wait_ge(g_ready, done_last(k, c + 1))
                for z in range(4):
                    if exists(k, c + 1):
                        pe.wait_ge(s_sub, done(k, c + 1, per=4, more=z + 1))
                    else:
                        pe.wait_ge(s_sub, done(k, c, per=4, more=z + 1))
                    for g in range(2 * z, min(2 * z + 2, TRI)):
                        to = z * 512 + (g % 2) * 3 * T
                        _, at = chunk(0, g)
                        pe.matmul(ps_s[:, to:to + 2 * T], probs_t[c % 2][:, at:at + S], gram[b][:, 0:2 * T],
                                  start=g % 2 == 0, stop=False, skip_group_check=True)
                        _, at = chunk(1, g)
                        n = (2 if g == TRI - 1 else 3) * T - T - G2
                        to += T + G2
                        ins = pe.matmul(ps_s[:, to:to + n], probs_t[c % 2][:, at:at + S],
                                        gram[b][:, 2 * T:2 * T + n],
                                        start=False, stop=True, skip_group_check=True)
                    ins.then_inc(w_psum, 1)

            def turn_back(k, c):
                pe.wait_ge(u_evac, done(k, c + 1))
                if exists(k, c - 1) and last(c - 1):
                    pe.wait_ge(x_ready, done(k, c))
                for i in range(2):
                    ins = pe.transpose(ps_c[:, i * S:(i + 1) * S], u_sb[:, i * S:(i + 1) * S], ident[:, :])
                ins.then_inc(ut_psum, 1)

            def turn_image(k, c):
                pe.wait_ge(u_evac, done(k, c + 2 if exists(k, c + 1) else c + 1))
                pe.wait_ge(pip_ready, done_last(k, c + 1))
                pe.wait_ge(pipt_evac, done_last(k, c))
                pe.transpose(ps_c[0:H * NIP, 2 * S:3 * S], p_ip[:, :], ident[:, :]).then_inc(pipt_psum, 1)

            def turn_out(k, c):
                b = c % NB
                pe.wait_ge(o_ready, done(k, c + 1))
                if last(c):
                    pe.wait_ge(pipt_evac, done_last(k, c + 1))
                for m in range(2):
                    ins = pe.matmul(ps_c[0:HC, m * S:(m + 1) * S], o_sb[c % 2][:, m * HC:(m + 1) * HC], ident[:, :],
                                    is_transpose=True, start=True, stop=not last(c))
                    if last(c):
                        ins = pe.matmul(ps_c[0:HC, m * S:(m + 1) * S], v_ip[b][:, m * HC:(m + 1) * HC],
                                        p_ip_t[:, :], start=False, stop=True)
                ins.then_inc(ot_psum, 1)

            def project_out(k, c):
                l = layer(c)
                pe.wait_ge(ot_evac, done(k, c + 1))
                for m in range(2):
                    for kt in range(2):
                        ins = pe.matmul(ps_c[0:HC, m * S:(m + 1) * S], w_half(wo, l, kt, m * HC, HC),
                                        o_t[:, kt * S:(kt + 1) * S], start=kt == 0, stop=kt == 1)
                ins.then_inc(y_psum, 1)

            def step_plain(k, c):
                scores_early = early(k, c)
                if not scores_early:
                    scores(k, c, 0)
                    scores(k, c, 1)
                queries(k, c + 1)
                if deferred(c - 2):
                    for w in range(4):
                        product(k, c - 2, w)
                turn(k, c - 1, 0)
                scores(k, c, 2)
                scores(k, c, 3)
                turn_back(k, c - 2)
                values(k, c + 1)
                turn(k, c - 1, 1)
                turn(k, c - 1, 2)
                turn_out(k, c - 2)
                keys(k, c + 2)
                project_out(k, c - 2)
                turn(k, c - 1, 3)
                scores(k, c + 1, 0)
                scores(k, c + 1, 1)
                if not deferred(c - 1):
                    for w in range(4):
                        product(k, c - 1, w)

            def step(k, c):
                if plain(c):
                    step_plain(k, c)
                    return
                now, prev, out, nxt = exists(k, c), exists(k, c - 1), exists(k, c - 2), exists(k, c + 1)
                late = exists(k, c - 3) and last(c - 3)
                soon = out and not last(c - 2)
                if now and not early(k, c):
                    scores(k, c, 0)
                    scores(k, c, 1)
                if nxt:
                    queries(k, c + 1)
                if out and not late:
                    turn_back(k, c - 2)
                if now:
                    scores(k, c, 2)
                    scores(k, c, 3)
                if prev:
                    turn(k, c - 1, 0)
                    turn(k, c - 1, 1)
                if late and not final(k, c):
                    turn_image(k, c - 3)
                if prev:
                    turn(k, c - 1, 2)
                if nxt:
                    values(k, c + 1)
                if final(k, c) and prev:
                    turn(k, c - 1, 3)
                if final(k, c):
                    turn_image(k, c - 3)
                if late:
                    turn_out(k, c - 3)
                    project_out(k, c - 3)
                if final(k, c) and exists(k, c + 2):
                    keys(k, c + 2)
                if late and out:
                    turn_back(k, c - 2)
                if soon:
                    turn_out(k, c - 2)
                if nxt and last(c + 1) and prev:
                    turn(k, c - 1, 3)
                if nxt and last(c + 1):
                    image(k, c + 1)
                if exists(k, c + 2) and not last(c + 1) and not final(k, c):
                    keys(k, c + 2)
                if soon:
                    project_out(k, c - 2)
                if prev and not final(k, c) and not (nxt and last(c + 1)):
                    turn(k, c - 1, 3)
                if nxt and early(k, c + 1):
                    scores(k, c + 1, 0)
                    scores(k, c + 1, 1)
                if exists(k, c + 2) and last(c + 1) and not last(c - 1):
                    keys(k, c + 2)
                if prev:
                    for w in range(4):
                        product(k, c - 1, w)
                if exists(k, c + 2) and last(c + 1) and last(c - 1):
                    keys(k, c + 2)
                if prev and last(c - 1):
                    gram_product(k, c - 1)

            pe.wait_ge(ld_w, N_LD)
            pe.wait_ge(setup, N_SET)
            pe.wait_ge(setup_pool, N_SET_POOL)
            keys(0, 0)
            queries(0, 0)
            values(0, 0)
            keys(0, 1)
            run(pe, step)

        @block.scalar
        def _(act):
            act.wait_ge(setup, N_SET)
            for n, (tile, src) in enumerate(WEIGHTS):
                act.dma_start(tile, src).then_inc(ld_w, 16)
            act.dma_start(wo[96:97, :], a["bias"]).then_inc(ld_w, 16)
            for b in range(NB):
                act.dma_start(v_rows[b][:, :], a["v_fixed"]).then_inc(ld_w, 16)
            act.wait_ge(ld_w, N_LD)

            def keys(k, c):
                act.wait_ge(k_psum, done(k, c + 1))
                act.wait_ge(k_ready, done(k, c - 1, per=4))
                act.wait_ge(k_moved, done(k, c, per=16 * 4))
                for to in (0, 64):
                    act.activation(k_stack[c % 2][to:to + CQ, 0:2 * T], ps_p[0:CQ, 0:2 * T], ACT.Copy)
                    ins = act.activation(k_stack[c % 2][to:to + CQ, 2 * T:4 * T], ps_p[64:64 + CQ, 0:2 * T], ACT.Copy)
                ins.then_inc(k_evac, 1)

            def queries(k, c):
                act.wait_ge(q_psum, done(k, c + 1))
                act.activation(q_stack[c % 2][:, 0:2 * S], ps_p[0:QROWS, 0:2 * S], ACT.Copy)
                act.activation(q_stack[c % 2][64:64 + CQ, 2 * S:4 * S], ps_p[64:64 + CQ, 0:2 * S],
                               ACT.Copy).then_inc(q_evac, 1)

            def exps(k, c, q):
                act.wait_ge(s_sub, done(k, c, per=4, more=q + 1))
                n = TXT if last(c) else T
                p = probs[c % 2][:, q * QC:(q + 1) * QC].rearrange("p (h t) -> p h t", t=T)[:, :, 0:n]
                act.activation(p, p, ACT.Exp, scale=SCALE).then_inc(p_ready, 1)

            def turned(k, c, w):
                kind, gs = PWAVES[w]
                act.wait_ge(t_psum, done(k, c, per=4, more=w + 1))
                if w == 0:
                    act.wait_ge(u_psum, done(k, c - 1))
                    if last(c - 2) and exists(k, c - 2):
                        act.wait_ge(w_psum, done_last(k, c - 1, per=4))
                _, at = chunk(kind, gs[0])
                n = len(gs) * S
                act.activation(probs_t[c % 2][:, at:at + n], ps_t[:, (w % 2) * 512:(w % 2) * 512 + n],
                               ACT.Copy).then_inc(t_evac, 1)

            def products(k, c):
                act.wait_ge(u_psum, done(k, c + 1))
                act.wait_ge(ut_psum, done(k, c))
                act.activation(u_sb[:, :], ps_c[:, 0:2 * S], ACT.Copy).then_inc(u_evac, 1)

            def image_exp(k, c):
                act.wait_ge(ip_step, done_last(k, c, per=IP_STEPS, more=19))
                act.activation(f_exp[:, :], f_sub[:, :], ACT.Exp, scale=0.5).then_inc(fe_ready, 1)

            def image_turned(k, c):
                act.wait_ge(pipt_psum, done_last(k, c + 1))
                act.wait_ge(ot_psum, done(k, c))
                act.activation(p_ip_t[:, :], ps_c[0:H * NIP, 2 * S:3 * S], ACT.Copy).then_inc(pipt_evac, 1)

            def results(k, c):
                act.wait_ge(ot_psum, done(k, c + 1))
                act.wait_ge(y_psum, done(k, c))
                act.activation(o_t[0:HC, :], ps_c[0:HC, 0:2 * S], ACT.Copy).then_inc(ot_evac, 1)

            def step_plain(k, c):
                queries(k, c + 1)
                exps(k, c, 0)
                products(k, c - 2)
                turned(k, c - 1, 0)
                exps(k, c, 1)
                turned(k, c - 1, 1)
                results(k, c - 2)
                turned(k, c - 1, 2)
                keys(k, c + 2)
                exps(k, c, 2)
                turned(k, c - 1, 3)
                exps(k, c, 3)

            def step(k, c):
                if plain(c):
                    step_plain(k, c)
                    return
                now, prev, out, nxt = exists(k, c), exists(k, c - 1), exists(k, c - 2), exists(k, c + 1)
                late = exists(k, c - 3) and last(c - 3)
                soon = out and not last(c - 2)
                if out:
                    products(k, c - 2)
                if nxt:
                    queries(k, c + 1)
                if now and not late:
                    exps(k, c, 0)
                if prev:
                    turned(k, c - 1, 0)
                    turned(k, c - 1, 1)
                if late:
                    if final(k, c):
                        image_exp(k, c - 3)
                        if prev:
                            turned(k, c - 1, 2)
                    image_turned(k, c - 3)
                    if now:
                        exps(k, c, 0)
                    if prev and final(k, c):
                        turned(k, c - 1, 3)
                    if prev and not final(k, c):
                        turned(k, c - 1, 2)
                    results(k, c - 3)
                if now:
                    exps(k, c, 1)
                if prev and not late:
                    turned(k, c - 1, 2)
                if final(k, c) and exists(k, c + 2):
                    keys(k, c + 2)
                if soon:
                    results(k, c - 2)
                if exists(k, c + 2) and not last(c + 1) and not final(k, c):
                    keys(k, c + 2)
                if prev and not final(k, c):
                    turned(k, c - 1, 3)
                if now:
                    exps(k, c, 2)
                if exists(k, c + 2) and last(c + 1):
                    keys(k, c + 2)
                if now:
                    exps(k, c, 3)
                if out and last(c - 2) and not final(k, c + 1):
                    image_exp(k, c - 2)

            keys(0, 0)
            queries(0, 0)
            keys(0, 1)
            run(act, step)

        @block.vector
        def _(dve):
            zeros = [wq, wo, o_t, u_sb] + x_in + x_work
            sets = 0
            for tile in zeros:
                dve.memset(tile[:, :], 0.0).then_inc(setup, 1)
                sets += 1
            dve.memset(ps_c[:, :], 0.0).then_inc(setup, 1)
            dve.wait_ge(setup, sets + 1)
            dve.memset(o_t[96:97, 0:S], 1.0).then_inc(setup, 1)
            dve.memset(ones[:, :], 1.0).then_inc(setup, 1)
            assert sets + 3 == N_SET
            for i, s in enumerate(primed):
                dve.memset(z_a[:, i:i + 1], 0.0).then_inc(s, 1)
            dve.wait_ge(setup_pool, N_SET_POOL)
            dve.wait_ge(ld_w, N_LD)

            def top_of(k, c, q):
                dve.wait_ge(s_psum, done(k, c, per=4, more=q + 1))
                n = TXT if last(c) else T
                s = ps_s[:, q * 512:q * 512 + QC].rearrange("p (h t) -> p h t", t=T)
                at = (c % 2) * H + q * QH
                dve.tensor_reduce(top[:, at:at + QH], s[:, :, 0:n], AX.X, ALU.max).then_inc(s_top, 1)

            def less_top(k, c, q):
                n = TXT if last(c) else T
                s = ps_s[:, q * 512:q * 512 + QC].rearrange("p (h t) -> p h t", t=T)
                p = probs[c % 2][:, q * QC:(q + 1) * QC].rearrange("p (h t) -> p h t", t=T)
                at = (c % 2) * H + q * QH
                if q == 0:
                    dve.wait_ge(t_psum, done(k, c - 1, per=4))
                if last(c):
                    dve.tensor_copy(s_ip[c % NB][:, q * QH * NIP:(q + 1) * QH * NIP]
                                    .rearrange("p (h t) -> p h t", t=NIP), s[:, :, n:T])
                dve.wait_ge(s_top, done(k, c, per=4, more=q + 1))
                dve.tensor_tensor(p[:, :, 0:n], s[:, :, 0:n],
                                  top[:, at:at + QH].unsqueeze(2).to_broadcast([128, QH, n]),
                                  ALU.subtract).then_inc(s_sub, 1)

            def keys_low(k, c):
                dve.wait_ge(k_evac, done(k, c + 1))
                for q, lo in enumerate((0, 64)):
                    ins = dve.tensor_tensor(k_low[lo:lo + CQ, :], ps_p[lo:lo + CQ, 0:2 * T],
                                            k_stack[c % 2][lo:lo + CQ, q * 2 * T:(q + 1) * 2 * T].bitcast(F32),
                                            ALU.subtract)
                ins.then_inc(k_split, 1)

            def queries_low(k, c):
                dve.wait_ge(q_evac, done(k, c + 1))
                for q, lo in enumerate((0, 64)):
                    cols = slice(q * 2 * S, (q + 1) * 2 * S)
                    ins = dve.tensor_tensor(q_stack[c % 2][64 - lo:64 - lo + CQ, cols], ps_p[lo:lo + CQ, 0:2 * S],
                                            q_stack[c % 2][lo:lo + CQ, cols].bitcast(F32), ALU.subtract)
                ins.then_inc(q_split, 1)

            def values(k, c):
                b = c % NB
                dve.wait_ge(v_psum, done(k, c + 1))
                dve.wait_ge(u_psum, done(k, c - NB + 1))
                n = TRI * 2 * D
                for kind in range(2):
                    v = v_rows[b][:, kind * TRI * UC:(kind + 1) * TRI * UC].rearrange("p (g u) -> p g u", u=UC)
                    m = mask_v[:, kind * 2 * D:(kind + 1) * 2 * D].unsqueeze(1).to_broadcast([128, TRI, 2 * D])
                    ins = dve.tensor_tensor(v[:, :, kind * D:kind * D + 2 * D],
                                            ps_p[:, kind * n:(kind + 1) * n].rearrange("p (g u) -> p g u", g=TRI),
                                            m, ALU.mult)
                ins.then_inc(v_ready, 1)

            def image_squares(k, c):
                b = c % NB
                dve.wait_ge(g_psum, done_last(k, c))
                s = context[b][:, :].rearrange("p (a n) -> p a n", a=2)[:, :, TXT:T]
                dve.tensor_tensor(ip_sq[:, :].rearrange("p (a n) -> p a n", a=2), s, s, ALU.mult)\
                   .then_inc(sq_ready, 1)

            def image_products(b):
                dve.tensor_tensor(gram[b][:, 0:2 * T].rearrange("p (h t) -> p h t", t=T),
                                  ps_p[:, 0:T].unsqueeze(1).to_broadcast([128, 2, T]),
                                  mask_g[:, 0:2 * T].rearrange("p (h t) -> p h t", t=T), ALU.mult)
                lo, mid = 2 * T, 3 * T - G2
                dve.tensor_tensor(gram[b][:, lo:mid], ps_p[:, T + G2:2 * T], mask_g[:, lo:mid], ALU.mult)
                dve.tensor_tensor(gram[b][:, mid:GC], ps_p[:, T:2 * T], mask_g[:, mid:GC], ALU.mult)\
                   .then_inc(g_ready, 1)

            def image(k, c):
                b = c % NB
                dve.wait_ge(g_psum, done_last(k, c + 1))
                at = 2 * T
                dve.tensor_scalar(ip_n2[b][:, :], ps_p[:, at:at + NIP], 1e-24, None, ALU.max)
                at += NIP + 2
                dve.tensor_tensor(v_ip[b][:, :], ps_p[0:H * NIP, at:at + C], mask_vip[:, :], ALU.mult)
                image_products(b)

            def weigh(k, c, z):
                lo, hi = 6 * z, min(6 * z + 6, H)
                if z == 0:
                    dve.wait_ge(p_marked, done_last(k, c + 1))
                dve.wait_ge(w_psum, done_last(k, c, per=4, more=z + 1))
                dve.tensor_tensor(weighted[:, lo * T:hi * T], ps_s[:, z * 512:z * 512 + (hi - lo) * T],
                                  probs[c % 2][:, lo * T:hi * T], ALU.mult).then_inc(w_ready, 1)

            def norms(k, c):
                dve.wait_ge(w_folded, done_last(k, c + 1))
                dve.tensor_reduce(q_n2[:, :], weighted[:, :].rearrange("p (h t) -> p h t", t=T)[:, :, 0:TXT - FOLD],
                                  AX.X, ALU.add).then_inc(qn_ready, 1)

            def results(k, c):
                u = ps_c[:, 0:TRI * 32].rearrange("p (g x) -> p g x", x=32)
                dve.wait_ge(ut_psum, done(k, c + 1))
                dve.reciprocal(recip[:, :].rearrange("p (g i) -> p g i", i=3), u[:, :, 3 * D:3 * D + 3])\
                   .then_inc(r_ready, 1)
                if last(c):
                    image_branch(k, c, 0)
                dve.wait_ge(r_ready, done(k, c + 1))
                dve.wait_ge(ot_psum, done(k, c - 1))
                ins = dve.tensor_tensor(o_sb[c % 2][:, :].rearrange("p (g i d) -> p g i d", i=3, d=D),
                                        u[:, :, 0:3 * D].rearrange("p g (i d) -> p g i d", d=D),
                                        recip[:, :].rearrange("p (g i) -> p g i", i=3).unsqueeze(3)
                                        .to_broadcast([128, TRI, 3, D]), ALU.mult)
                ins.then_inc(o_ready, 1)

            def image_branch(k, c, n):
                b = c % NB

                def per_head(ap):
                    return ap.unsqueeze(2).to_broadcast([128, H, NIP])

                def per_token(ap):
                    return ap[:, :].rearrange("p (h t) -> p h t", t=NIP)

                if n > 0:
                    dve.wait_ge(ip_step, done_last(k, c, per=IP_STEPS, more=n))
                y, y_new = rs_y[n // 3 % 2], rs_y[(n // 3 + 1) % 2]
                if n == 0:
                    u = ps_c[:, 0:TRI * 32].rearrange("p (g x) -> p g x", x=32)
                    dve.tensor_copy(den[:, :].rearrange("p (g i) -> p g i", i=3), u[:, :, 3 * D:3 * D + 3])\
                       .then_inc(ip_step, 1)
                    return
                if n == 1:
                    dve.wait_ge(w_ready, done_last(k, c + 1, per=4))
                    dve.tensor_copy(per_token(z_a),
                                    weighted[:, :].rearrange("p (h t) -> p h t", t=T)[:, :, TXT:T])
                    ins = dve.scalar_tensor_tensor(out=den2[:, :], in0=den[:, :], scalar=1e-24, in1=den[:, :],
                                                   op0=ALU.mult, op1=ALU.mult)
                elif n == 2:
                    dve.wait_ge(qn_ready, done_last(k, c + 1))
                    dve.tensor_copy(rs_x[:, H:H + NIP], ip_n2[b][:, :])
                    ins = dve.tensor_tensor(rs_x[:, 0:H], q_n2[:, :], den2[:, 0:H], ALU.max)
                elif n == 3:
                    ins = dve.tensor_scalar(rs_i[:, :], rs_x[:, :].bitcast(mybir.dt.int32), 1, None,
                                            ALU.logical_shift_right)
                elif n == 4:
                    ins = dve.tensor_scalar(rs_y[1][:, :], rs_i[:, :], -1.0, float(0x5F3759DF), ALU.mult, ALU.add)
                elif n < 14 and n % 3 == 2:
                    ins = dve.scalar_tensor_tensor(out=rs_t[:, :], in0=rs_x[:, :], scalar=-0.5,
                                                   in1=y[:, :].bitcast(F32), op0=ALU.mult, op1=ALU.mult)
                elif n < 14 and n % 3 == 0:
                    y = rs_y[(n // 3 - 1) % 2]
                    ins = dve.tensor_tensor(rs_u[:, :], rs_t[:, :], y[:, :].bitcast(F32), ALU.mult)
                elif n < 14:
                    y, y_new = rs_y[(n // 3 - 1) % 2], rs_y[n // 3 % 2]
                    ins = dve.scalar_tensor_tensor(out=y_new[:, :].bitcast(F32), in0=rs_u[:, :], scalar=1.5,
                                                   in1=y[:, :].bitcast(F32), op0=ALU.add, op1=ALU.mult)
                elif n == 14:
                    y = rs_y[0]
                    ins = dve.tensor_tensor(per_token(z_b), per_token(z_a), per_head(y[:, 0:H].bitcast(F32)), ALU.mult)
                elif n == 15:
                    y = rs_y[0]
                    ins = dve.tensor_tensor(per_token(z_c), per_token(z_b), y[:, H:H + NIP].bitcast(F32).unsqueeze(1)
                                            .to_broadcast([128, H, NIP]), ALU.mult)
                elif n == 16:
                    ins = dve.scalar_tensor_tensor(out=fused[:, :], in0=s_ip[b][:, :], scalar=2.0 * SCALE,
                                                   in1=z_c[:, :], op0=ALU.mult, op1=ALU.add)
                elif n == 17:
                    ins = dve.tensor_reduce(f_top[:, :], per_token(fused), AX.X, ALU.max)
                elif n == 18:
                    dve.wait_ge(fe_ready, done_last(k, c))
                    ins = dve.tensor_tensor(per_token(f_sub), per_token(fused), per_head(f_top[:, :]), ALU.subtract)
                elif n == 19:
                    dve.wait_ge(fe_ready, done_last(k, c + 1))
                    ins = dve.tensor_reduce(f_sum[:, :], per_token(f_exp), AX.X, ALU.add)
                elif n == 20:
                    ins = dve.reciprocal(f_rec[:, :], f_sum[:, :])
                ins.then_inc(ip_step, 1)

            def image_weights(k, c):
                dve.wait_ge(ip_step, done_last(k, c + 1, per=IP_STEPS))
                dve.wait_ge(pipt_psum, done_last(k, c))
                f = f_rec[:, :].unsqueeze(2).to_broadcast([128, H, NIP])
                dve.scalar_tensor_tensor(out=p_ip[:, :].rearrange("p (h t) -> p h t", t=NIP),
                                         in0=f_exp[:, :].rearrange("p (h t) -> p h t", t=NIP),
                                         scalar=fside[:, 0:1], in1=f, op0=ALU.mult, op1=ALU.mult)\
                   .then_inc(pip_ready, 1)

            def new_x(k, c):
                l, b = layer(c), c % NB
                dve.wait_ge(y_psum, done(k, c + 1))
                old = x_in[b] if l == 0 else x_work[b]
                to = x_out[b] if l == L - 1 else x_work[b]
                if l == L - 1:
                    n = c // STEPS * 16
                    if isinstance(k, int):
                        n += k * 16
                        if n > 0:
                            dve.wait_ge(st_x[b], n)
                    else:
                        dve.wait_ge(st_x[b], k * 16 + n)
                dve.tensor_tensor(to[0:HC, :], ps_c[0:HC, 0:2 * S], old[0:HC, :], ALU.add).then_inc(x_ready, 1)

            def step_plain(k, c):
                top_of(k, c, 0)
                less_top(k, c, 0)
                top_of(k, c, 1)
                queries_low(k, c + 1)
                less_top(k, c, 1)
                top_of(k, c, 2)
                results(k, c - 2)
                values(k, c + 1)
                less_top(k, c, 2)
                top_of(k, c, 3)
                less_top(k, c, 3)
                new_x(k, c - 2)
                keys_low(k, c + 2)

            def step(k, c):
                if plain(c):
                    step_plain(k, c)
                    return
                now, prev, out, nxt = exists(k, c), exists(k, c - 1), exists(k, c - 2), exists(k, c + 1)
                late = exists(k, c - 3) and last(c - 3)
                fused = out and last(c - 2)

                def image_steps(lo, hi):
                    if fused:
                        for n in range(lo, hi):
                            image_branch(k, c - 2, n)

                def scored(q):
                    if now:
                        top_of(k, c, q)
                        less_top(k, c, q)

                if late:
                    if nxt and not final(k, c):
                        queries_low(k, c + 1)
                    scored(0)
                    if now:
                        top_of(k, c, 1)
                    if nxt:
                        values(k, c + 1)
                    if now:
                        less_top(k, c, 1)
                    scored(2)
                    new_x(k, c - 3)
                    if now:
                        top_of(k, c, 3)
                    if out:
                        results(k, c - 2)
                    if fused:
                        norms(k, c - 2)
                    image_steps(1, 3)
                    if exists(k, c + 2):
                        keys_low(k, c + 2)
                    image_steps(3, 4)
                    if now:
                        less_top(k, c, 3)
                    image_steps(4, 7)
                    if out and not fused:
                        new_x(k, c - 2)
                else:
                    scored(0)
                    if now:
                        top_of(k, c, 1)
                    if nxt:
                        queries_low(k, c + 1)
                    if now:
                        less_top(k, c, 1)
                    if out:
                        results(k, c - 2)
                    if nxt:
                        values(k, c + 1)
                    if nxt and last(c + 1):
                        image_squares(k, c + 1)
                    if fused:
                        norms(k, c - 2)
                    image_steps(1, 3)
                    if now:
                        top_of(k, c, 2)
                    image_steps(3, 4)
                    if fused:
                        image(k, c + 1)
                    if now:
                        less_top(k, c, 2)
                    image_steps(4, 5)
                    if now:
                        top_of(k, c, 3)
                    image_steps(5, 6)
                    if nxt and last(c + 1) and not fused:
                        image(k, c + 1)
                    if out and not fused:
                        new_x(k, c - 2)
                    image_steps(6, 7)
                    if exists(k, c + 2) and not last(c + 1):
                        keys_low(k, c + 2)
                    if now:
                        less_top(k, c, 3)
                image_steps(7, 9)
                if exists(k, c + 2) and last(c + 1):
                    keys_low(k, c + 2)
                for z in range(4):
                    image_steps(9 + 2 * z, 11 + 2 * z)
                    if prev and last(c - 1):
                        weigh(k, c - 1, z)
                if final(k, c + 1) and exists(k, c + 2):
                    queries_low(k, c + 2)
                image_steps(17, 21)
                if fused:
                    image_weights(k, c - 2)

            keys_low(0, 0)
            queries_low(0, 0)
            values(0, 0)
            keys_low(0, 1)
            run(dve, step)

        @block.gpsimd
        def _(pool):
            for n in range(2):
                pool.memset(probs[n][:, :], 0.0).then_inc(setup_pool, 1)
                pool.memset(k_blocks[n][:, :].bitcast(F32), 0.0).then_inc(setup_pool, 1)
            pool.memset(no_ip[:, :], 0.0).then_inc(setup_pool, 1)
            pool.wait_ge(setup, N_SET)
            pool.wait_ge(setup_pool, N_SET_POOL)
            pool.wait_ge(ld_w, N_LD)

            def clear(k, c):
                pool.wait_ge(t_psum, done(k, c - 1, per=4))
                if last(c - 2) and exists(k, c - 2):
                    pool.wait_ge(w_ready, done_last(k, c - 1, per=4))
                z = no_ip[:, :].rearrange("p (h t) -> p h t", t=NIP)
                pool.tensor_tensor(probs[c % 2][:, 0:H * T].rearrange("p (h t) -> p h t", t=T)[:, :, TXT:T],
                                   z, z, ALU.mult).then_inc(p_clear, 1)

            def mark(k, c):
                pool.wait_ge(t_psum, done(k, c + 1, per=4))
                one = ones[:, 0:H * NIP].rearrange("p (h t) -> p h t", t=NIP)
                pool.tensor_tensor(probs[c % 2][:, 0:H * T].rearrange("p (h t) -> p h t", t=T)[:, :, TXT:T],
                                   one, one, ALU.mult).then_inc(p_marked, 1)

            def keys(k, c):
                pool.wait_ge(k_moved, done(k, c + 1, per=16 * 4))
                pool.wait_ge(s_psum, done(k, c - 1, per=4))
                for q in range(4):
                    at = (q % 2 * 2 + q // 2) * T
                    pool.tensor_tensor(k_blocks[c % 2][:, q * QE:q * QE + QC].rearrange("p (h t) -> p h t", t=T),
                                       k_stack[c % 2][:, at:at + T].bitcast(F32)
                                       .unsqueeze(1).to_broadcast([QROWS, QH, T]),
                                       mask_k[:, :].unsqueeze(2).to_broadcast([QROWS, QH, T]),
                                       ALU.mult).then_inc(k_ready, 1)

            def fold(k, c):
                pool.wait_ge(w_ready, done_last(k, c + 1, per=4))
                w = weighted[:, :].rearrange("p (h t) -> p h t", t=T)
                pool.tensor_tensor(w[:, :, 0:FOLD], w[:, :, 0:FOLD], w[:, :, TXT - FOLD:TXT], ALU.add)\
                    .then_inc(w_folded, 1)

            def step(k, c):
                if exists(k, c) and last(c):
                    clear(k, c)
                if exists(k, c - 1) and last(c - 1):
                    mark(k, c - 1)
                    fold(k, c - 1)
                if exists(k, c + 2):
                    keys(k, c + 2)

            keys(0, 0)
            keys(0, 1)
            run(pool, step)



def _halves(w, rows):
    return w.reshape(2, rows, w.shape[-1]).transpose(1, 0, 2)


def _layout(inputs):
    f = {k: np.asarray(v) for k, v in inputs.items()}
    n = {"q": ["L0_xattn_to_q_w", "L1_xattn_Wq", "L2_xattn_Wq", "L3_xattn_W_q"],
         "k": ["L0_xattn_to_k_w", "L1_xattn_Wk", "L2_xattn_Wk", "L3_xattn_W_k"],
         "v": ["L0_xattn_to_v_w", "L1_xattn_Wv", "L2_xattn_Wv", "L3_xattn_W_v"],
         "o": ["L0_xattn_to_out_w", "L1_xattn_Wout", "L2_xattn_Wo", "L3_xattn_W_out"],
         "b": ["L0_xattn_to_out_b", "L1_xattn_bout", "L2_xattn_bo", "L3_xattn_b_out"]}

    def weights(kind):
        return [f[name].T if l == 2 else f[name] for l, name in enumerate(n[kind])]

    out = {}
    x = f["x"]
    dt = x.dtype
    out["x"] = x.reshape(B, S, 2, HC).transpose(0, 3, 2, 1).reshape(B, HC, 2 * S)
    ct = f["ctx_2048"].reshape(B, T, 2, 128).transpose(0, 3, 2, 1)
    cx = np.zeros((B, 128, 2, CX), dt)
    for kind in range(2):
        toks = [t for _, t in rows_of(kind)]
        cx[:, :, :, kind * 128:kind * 128 + len(toks)] = ct[:, :, :, toks]
    cx[:, :, :, 256:] = ct[:, :, :, [TXT + i % NIP for i in range(H * NIP)]]
    out["ctx"] = cx.reshape(B, 128, 2 * CX)
    a, q_b = list(range(CQ)), list(range(CQ, HC))
    q_rows = a + a[:THIRD] + q_b + a[THIRD:]
    k_rows = q_rows[:KROWS]

    def rows(w, n, channels):
        return _halves(w, n).reshape(n, 2, 2, HC)[:, :, :, channels]

    out["wq"] = np.stack([rows(w, HC, q_rows) for w in weights("q")], 1).reshape(HC, -1)
    out["wo"] = np.stack([_halves(w, HC) for w in weights("o")], 1).reshape(HC, -1)
    out["wk"] = np.stack([rows(w, 128, k_rows) for w in weights("k")], 1).reshape(128, -1)
    out["wkip"] = rows(f["L3_xattn_W_k_ip"], 128, k_rows).reshape(128, -1)
    out["wvip"] = _halves(f["L3_xattn_W_v_ip"], 128).reshape(128, -1)
    wv = np.zeros((128, L, 2, 2, TRI, 2, D), dt)
    for l, w in enumerate(weights("v")):
        w = _halves(w, 128).reshape(128, 2, H, D)
        for kind in range(2):
            for g, pair in enumerate(heads_of(kind)):
                for i, h in enumerate(pair):
                    if h is not None:
                        wv[:, l, kind, :, g, i] = w[:, :, h]
    out["wv"] = wv.reshape(128, -1)
    bias = np.zeros((1, L, 2, C), dt)
    for l, name in enumerate(n["b"]):
        bias[0, l, 0] = f[name]
    out["bias"] = bias.reshape(1, -1)
    out["fside"] = f["fside_S_0"].reshape(S, 1)
    out["ident"] = np.eye(128, dtype=dt)
    out["mask_k"] = np.kron(np.eye(QH, dtype=dt), np.ones((D, 1), dt))[a + a[:THIRD] + a + a[THIRD:]]
    out["mask_vip"] = np.kron(np.eye(H, dtype=dt), np.ones((NIP, D), dt))
    mv = np.zeros((128, 2, 2, D), dt)
    mg = [np.zeros((128, 2, T), dt) for _ in range(2)]
    vf = np.zeros((128, 2, TRI, UC), dt)
    for kind in range(2):
        for r, (h, t) in enumerate(rows_of(kind)):
            mv[r, kind, h - kind] = 1
            if t < TXT:
                mg[kind][r, h - kind] = 1
                if kind == 0 and h == 1:
                    mg[kind][r, 1, CUT:TXT] = 2
            vf[r, kind, :, 3 * D + h] = 1
            if h == 1:
                vf[r, kind, TRI - 1, 3 * D + 2] = 1
    out["mask_v"] = mv.reshape(128, -1)
    out["mask_g"] = np.concatenate([mg[0].reshape(128, -1), mg[1].reshape(128, -1)[:, G2:]], 1)
    out["v_fixed"] = vf.reshape(128, -1)
    return {k: np.ascontiguousarray(v) for k, v in out.items()}


def kernel(**inputs):
    import concourse.bacc as bacc
    from concourse.bass_utils import run_bass_kernel_spmd

    nc = bacc.Bacc("TRN2", target_bir_lowering=False, num_devices=1)
    arrays, tensors = {}, {}
    for name, v in _layout(inputs).items():
        arrays[f"in_{name}"] = v
        tensors[name] = nc.dram_tensor(f"in_{name}", v.shape, mybir.dt.from_np(v.dtype), kind="ExternalInput").ap()
    tensors["out"] = nc.dram_tensor("out_x", (B, HC, 2 * S), F32, kind="ExternalOutput").ap()
    build(nc, tensors)
    r = run_bass_kernel_spmd(nc, [arrays], core_ids=[0])
    got = np.asarray(r.results[0]["out_x"])
    return np.ascontiguousarray(got.reshape(B, HC, 2, S).transpose(0, 3, 2, 1).reshape(B, S, C))
```
